# Optimizing a Trainium2 kernel written in Bass

```python
import numpy as np
import jax
import jax.numpy as jnp

def _softmax(x, axis=-1):
    return jax.nn.softmax(x, axis=axis)

def _gelu(x):
    return jax.nn.gelu(x, approximate=True)

def _silu(x):
    return jax.nn.silu(x)

def _sigmoid(x):
    return jax.nn.sigmoid(x)

def _layernorm(x, axis=-1, eps=1e-05):
    m = jnp.mean(x, axis=axis, keepdims=True)
    v = jnp.var(x, axis=axis, keepdims=True)
    return (x - m) / jnp.sqrt(v + eps)

def _scatter_add(tgt, idx, src, axis=0):
    return tgt.at[idx].add(src)

def _segment_sum(src, seg, n):
    return jax.ops.segment_sum(src, seg, n)
kernel_name = 'mk_gnn_resnorm_d2_gnn_r32_3bb84b'

def setup_inputs(seed: int=0):
    np.random.seed(seed)
    _w = jnp.asarray

    def _rec_inputs():
        import jax
        import jax.numpy as jnp
        _gk = jax.random.key(seed)
        x = -0.0001538 + 1 * jax.random.normal(jax.random.fold_in(_gk, 1), (256, 768), jnp.float32)
        src = jax.random.randint(jax.random.fold_in(_gk, 2), (4096,), 0, 256, jnp.int32)
        dst = jax.random.randint(jax.random.fold_in(_gk, 3), (4096,), 0, 256, jnp.int32)
        _o = jnp.argsort(dst, stable=True)
        src = src[_o]
        dst = dst[_o]
        return (x, src, dst)
    x, src, dst = _rec_inputs()

    def _L0_gnn_setup():
        import jax, jax.numpy as jnp
        import numpy as np
        N_NODES = 256
        N_EDGES = 1024
        D = 768
        H1 = 8
        NEG_SLOPE = 0.2

        def gat_conv(x, src, dst, W, a_src, a_dst, b, heads, out_ch):
            n = x.shape[0]
            h = (x @ W).reshape(n, heads, out_ch)
            alpha_src = jnp.einsum('nhc,hc->nh', h, a_src)
            alpha_dst = jnp.einsum('nhc,hc->nh', h, a_dst)
            e = jax.nn.leaky_relu(alpha_src[src] + alpha_dst[dst], NEG_SLOPE)
            m = jax.ops.segment_max(e, dst, num_segments=n)
            m = jnp.where(jnp.isfinite(m), m, 0.0)
            p = jnp.exp(e - m[dst])
            denom = jax.ops.segment_sum(p, dst, num_segments=n)
            alpha = p / denom[dst]
            msg = h[src] * alpha[:, :, None]
            out = jax.ops.segment_sum(msg, dst, num_segments=n)
            return out.reshape(n, heads * out_ch) + b
        key = jax.random.key(seed)
        ks = jax.random.split(key, 10)
        s = 0.02
        x = jax.random.normal(ks[0], (N_NODES, D), dtype=jnp.float32)
        edge_index = jax.random.randint(ks[1], (2, N_EDGES), 0, N_NODES, dtype=jnp.int64)
        W1 = jax.random.normal(ks[2], (D, H1 * D), dtype=jnp.float32) * s
        a_src1 = jax.random.normal(ks[3], (H1, D), dtype=jnp.float32) * s
        a_dst1 = jax.random.normal(ks[4], (H1, D), dtype=jnp.float32) * s
        b1 = jnp.zeros((H1 * D,), dtype=jnp.float32)
        W2 = jax.random.normal(ks[5], (H1 * D, D), dtype=jnp.float32) * s
        a_src2 = jax.random.normal(ks[6], (1, D), dtype=jnp.float32) * s
        a_dst2 = jax.random.normal(ks[7], (1, D), dtype=jnp.float32) * s
        b2 = jnp.zeros((D,), dtype=jnp.float32)
        return {'x': x, 'edge_index': edge_index, 'W1': W1, 'a_src1': a_src1, 'a_dst1': a_dst1, 'b1': b1, 'W2': W2, 'a_src2': a_src2, 'a_dst2': a_dst2, 'b2': b2}
    _L0_gnn_all = _L0_gnn_setup()
    _L0_gnn_in = {k: v for k, v in _L0_gnn_all.items() if k in ('W1', 'a_src1', 'a_dst1', 'b1', 'W2', 'a_src2', 'a_dst2', 'b2')}
    del _L0_gnn_all

    def _L1_gnn_setup():
        import jax, jax.numpy as jnp
        import numpy as np
        N_NODES = 625
        N_EDGES = 5000
        IN_DIM = 768
        HID = 256
        HEADS = 4
        OUT_DIM = 768
        LN_EPS = 1e-05

        def _add_self_loops(edge_index, n):
            loop = jnp.arange(n, dtype=edge_index.dtype)
            return jnp.concatenate([edge_index, jnp.stack([loop, loop])], axis=1)

        def gat_conv(x, edge_index, W, a_src, a_dst, bias, heads, out_ch, concat):
            n = x.shape[0]
            ei = _add_self_loops(edge_index, n)
            src, dst = (ei[0], ei[1])
            xl = (x @ W).reshape(n, heads, out_ch)
            alpha_src = jnp.einsum('nhc,hc->nh', xl, a_src)
            alpha_dst = jnp.einsum('nhc,hc->nh', xl, a_dst)
            e = jax.nn.leaky_relu(alpha_src[src] + alpha_dst[dst], 0.2)
            m = jax.ops.segment_max(e, dst, num_segments=n)
            e = jnp.exp(e - m[dst])
            s = jax.ops.segment_sum(e, dst, num_segments=n)
            alpha = e / (s[dst] + 1e-16)
            msg = xl[src] * alpha[:, :, None]
            out = jax.ops.segment_sum(msg, dst, num_segments=n)
            out = out.reshape(n, heads * out_ch) if concat else out.mean(axis=1)
            return out + bias

        def layer_norm(x, g, b):
            mu = jnp.mean(x, axis=-1, keepdims=True)
            var = jnp.var(x, axis=-1, keepdims=True)
            return (x - mu) * jax.lax.rsqrt(var + LN_EPS) * g + b
        key = jax.random.key(seed)
        ks = jax.random.split(key, 16)
        s = 0.02
        HC = HID * HEADS
        return {'x': jax.random.normal(ks[0], (N_NODES, IN_DIM), jnp.float32), 'edge_index': jax.random.randint(ks[1], (2, N_EDGES), 0, N_NODES, jnp.int64 if jax.config.jax_enable_x64 else jnp.int32), 'W1': jax.random.normal(ks[2], (IN_DIM, HC), jnp.float32) * s, 'a_src1': jax.random.normal(ks[3], (HEADS, HID), jnp.float32) * s, 'a_dst1': jax.random.normal(ks[4], (HEADS, HID), jnp.float32) * s, 'b1': jnp.zeros((HC,), jnp.float32), 'g1': jnp.ones((HC,), jnp.float32), 'be1': jnp.zeros((HC,), jnp.float32), 'Wr1': jax.random.normal(ks[5], (IN_DIM, HC), jnp.float32) * s, 'br1': jnp.zeros((HC,), jnp.float32), 'W2': jax.random.normal(ks[6], (HC, OUT_DIM), jnp.float32) * s, 'a_src2': jax.random.normal(ks[7], (1, OUT_DIM), jnp.float32) * s, 'a_dst2': jax.random.normal(ks[8], (1, OUT_DIM), jnp.float32) * s, 'b2': jnp.zeros((OUT_DIM,), jnp.float32), 'g2': jnp.ones((OUT_DIM,), jnp.float32), 'be2': jnp.zeros((OUT_DIM,), jnp.float32), 'Wr2': jax.random.normal(ks[9], (HC, OUT_DIM), jnp.float32) * s, 'br2': jnp.zeros((OUT_DIM,), jnp.float32)}
    _L1_gnn_all = _L1_gnn_setup()
    _L1_gnn_in = {k: v for k, v in _L1_gnn_all.items() if k in ('W1', 'a_src1', 'a_dst1', 'b1', 'g1', 'be1', 'Wr1', 'br1', 'W2', 'a_src2', 'a_dst2', 'b2', 'g2', 'be2', 'Wr2', 'br2')}
    del _L1_gnn_all
    return {'x': x, 'src': src, 'dst': dst, 'L0_gnn_W1': _L0_gnn_in['W1'], 'L0_gnn_a_src1': _L0_gnn_in['a_src1'], 'L0_gnn_a_dst1': _L0_gnn_in['a_dst1'], 'L0_gnn_b1': _L0_gnn_in['b1'], 'L0_gnn_W2': _L0_gnn_in['W2'], 'L0_gnn_a_src2': _L0_gnn_in['a_src2'], 'L0_gnn_a_dst2': _L0_gnn_in['a_dst2'], 'L0_gnn_b2': _L0_gnn_in['b2'], 'L1_gnn_W1': _L1_gnn_in['W1'], 'L1_gnn_a_src1': _L1_gnn_in['a_src1'], 'L1_gnn_a_dst1': _L1_gnn_in['a_dst1'], 'L1_gnn_b1': _L1_gnn_in['b1'], 'L1_gnn_g1': _L1_gnn_in['g1'], 'L1_gnn_be1': _L1_gnn_in['be1'], 'L1_gnn_Wr1': _L1_gnn_in['Wr1'], 'L1_gnn_br1': _L1_gnn_in['br1'], 'L1_gnn_W2': _L1_gnn_in['W2'], 'L1_gnn_a_src2': _L1_gnn_in['a_src2'], 'L1_gnn_a_dst2': _L1_gnn_in['a_dst2'], 'L1_gnn_b2': _L1_gnn_in['b2'], 'L1_gnn_g2': _L1_gnn_in['g2'], 'L1_gnn_be2': _L1_gnn_in['be2'], 'L1_gnn_Wr2': _L1_gnn_in['Wr2'], 'L1_gnn_br2': _L1_gnn_in['br2']}

def reference(x, src, dst, L0_gnn_W1, L0_gnn_a_src1, L0_gnn_a_dst1, L0_gnn_b1, L0_gnn_W2, L0_gnn_a_src2, L0_gnn_a_dst2, L0_gnn_b2, L1_gnn_W1, L1_gnn_a_src1, L1_gnn_a_dst1, L1_gnn_b1, L1_gnn_g1, L1_gnn_be1, L1_gnn_Wr1, L1_gnn_br1, L1_gnn_W2, L1_gnn_a_src2, L1_gnn_a_dst2, L1_gnn_b2, L1_gnn_g2, L1_gnn_be2, L1_gnn_Wr2, L1_gnn_br2):
    import jax
    import jax.numpy as jnp

    def _L0_gnn_ref(x, edge_index, W1, a_src1, a_dst1, b1, W2, a_src2, a_dst2, b2):
        import jax, jax.numpy as jnp
        import numpy as np
        N_NODES = 256
        N_EDGES = 1024
        D = 768
        H1 = 8
        NEG_SLOPE = 0.2

        def gat_conv(x, src, dst, W, a_src, a_dst, b, heads, out_ch):
            n = x.shape[0]
            h = (x @ W).reshape(n, heads, out_ch)
            alpha_src = jnp.einsum('nhc,hc->nh', h, a_src)
            alpha_dst = jnp.einsum('nhc,hc->nh', h, a_dst)
            e = jax.nn.leaky_relu(alpha_src[src] + alpha_dst[dst], NEG_SLOPE)
            m = jax.ops.segment_max(e, dst, num_segments=n)
            m = jnp.where(jnp.isfinite(m), m, 0.0)
            p = jnp.exp(e - m[dst])
            denom = jax.ops.segment_sum(p, dst, num_segments=n)
            alpha = p / denom[dst]
            msg = h[src] * alpha[:, :, None]
            out = jax.ops.segment_sum(msg, dst, num_segments=n)
            return out.reshape(n, heads * out_ch) + b
        n = x.shape[0]
        loops = jnp.arange(n, dtype=edge_index.dtype)
        src = jnp.concatenate([edge_index[0], loops])
        dst = jnp.concatenate([edge_index[1], loops])
        h = gat_conv(x, src, dst, W1, a_src1, a_dst1, b1, H1, D)
        h = jax.nn.elu(h)
        out = gat_conv(h, src, dst, W2, a_src2, a_dst2, b2, 1, D)
        return out

    def _L1_gnn_ref(x, edge_index, W1, a_src1, a_dst1, b1, g1, be1, Wr1, br1, W2, a_src2, a_dst2, b2, g2, be2, Wr2, br2):
        import jax, jax.numpy as jnp
        import numpy as np
        N_NODES = 625
        N_EDGES = 5000
        IN_DIM = 768
        HID = 256
        HEADS = 4
        OUT_DIM = 768
        LN_EPS = 1e-05

        def _add_self_loops(edge_index, n):
            loop = jnp.arange(n, dtype=edge_index.dtype)
            return jnp.concatenate([edge_index, jnp.stack([loop, loop])], axis=1)

        def gat_conv(x, edge_index, W, a_src, a_dst, bias, heads, out_ch, concat):
            n = x.shape[0]
            ei = _add_self_loops(edge_index, n)
            src, dst = (ei[0], ei[1])
            xl = (x @ W).reshape(n, heads, out_ch)
            alpha_src = jnp.einsum('nhc,hc->nh', xl, a_src)
            alpha_dst = jnp.einsum('nhc,hc->nh', xl, a_dst)
            e = jax.nn.leaky_relu(alpha_src[src] + alpha_dst[dst], 0.2)
            m = jax.ops.segment_max(e, dst, num_segments=n)
            e = jnp.exp(e - m[dst])
            s = jax.ops.segment_sum(e, dst, num_segments=n)
            alpha = e / (s[dst] + 1e-16)
            msg = xl[src] * alpha[:, :, None]
            out = jax.ops.segment_sum(msg, dst, num_segments=n)
            out = out.reshape(n, heads * out_ch) if concat else out.mean(axis=1)
            return out + bias

        def layer_norm(x, g, b):
            mu = jnp.mean(x, axis=-1, keepdims=True)
            var = jnp.var(x, axis=-1, keepdims=True)
            return (x - mu) * jax.lax.rsqrt(var + LN_EPS) * g + b
        h0 = x
        h = gat_conv(x, edge_index, W1, a_src1, a_dst1, b1, HEADS, HID, True)
        h = layer_norm(h, g1, be1)
        h = jax.nn.relu(h)
        h = h + (h0 @ Wr1 + br1)
        h1 = h
        h = gat_conv(h, edge_index, W2, a_src2, a_dst2, b2, 1, OUT_DIM, False)
        h = layer_norm(h, g2, be2)
        h = h + (h1 @ Wr2 + br2)
        return h
    edge_index = jnp.stack([src, dst])
    x = _layernorm(x + _L0_gnn_ref(x, edge_index, L0_gnn_W1, L0_gnn_a_src1, L0_gnn_a_dst1, L0_gnn_b1, L0_gnn_W2, L0_gnn_a_src2, L0_gnn_a_dst2, L0_gnn_b2), axis=-1)
    x = _layernorm(x + _L1_gnn_ref(x, edge_index, L1_gnn_W1, L1_gnn_a_src1, L1_gnn_a_dst1, L1_gnn_b1, L1_gnn_g1, L1_gnn_be1, L1_gnn_Wr1, L1_gnn_br1, L1_gnn_W2, L1_gnn_a_src2, L1_gnn_a_dst2, L1_gnn_b2, L1_gnn_g2, L1_gnn_be2, L1_gnn_Wr2, L1_gnn_br2), axis=-1)
    return x

_drawn_inputs = setup_inputs


def setup_inputs(seed=0):
    import zlib

    import numpy as np

    out = dict(_drawn_inputs(seed))
    spreads = {'L0_gnn_b1': (0.0, 0.1),
     'L0_gnn_b2': (0.0, 0.1),
     'L1_gnn_b1': (0.0, 0.1),
     'L1_gnn_g1': (1.0, 0.2),
     'L1_gnn_be1': (0.0, 0.1),
     'L1_gnn_br1': (0.0, 0.1),
     'L1_gnn_b2': (0.0, 0.1),
     'L1_gnn_g2': (1.0, 0.2),
     'L1_gnn_be2': (0.0, 0.1),
     'L1_gnn_br2': (0.0, 0.1)}
    factors = {'L0_gnn_a_dst1': 8.0,
     'L0_gnn_a_src2': 8.0,
     'L0_gnn_a_dst2': 8.0,
     'L1_gnn_a_dst1': 5.479,
     'L1_gnn_a_src2': 2.805,
     'L1_gnn_a_dst2': 4.924}
    for name, (base, spread) in spreads.items():
        noise = np.random.default_rng([zlib.crc32(name.encode()), seed]).standard_normal(out[name].shape)
        drawn = base * np.exp(spread * noise) if base else spread * noise
        out[name] = jnp.asarray(drawn.astype(out[name].dtype))
    for name, factor in factors.items():
        out[name] = (out[name] * factor).astype(out[name].dtype)
    return out
```

```python
from contextlib import ExitStack

import concourse.bass as bass
from concourse import mybir

ALU = mybir.AluOpType
ACT = mybir.ActivationFunctionType
F32 = mybir.dt.float32
F32R = mybir.dt.float32r
BF16 = mybir.dt.bfloat16
I32 = mybir.dt.int32

P = 128
N = 256
NT = N // P
D = 768
KD = D // P
H0 = 8
H1, C1 = 4, 256
HC = H1 * C1
KH = HC // P
E = 4096
ET = E // P
BANK = 512
SLOPE = 0.2
EPS = 1e-5
FAR = -1.0e30

CH = KD
RG = 3
POOL_CH = 4
DVE_CH = CH - POOL_CH
PHASES = 2 * H0

A_CONV2, A_GAT1, A_GAT2 = H0, H0 + 1, H0 + 2


def block1_plan():
    plan = []
    pool, dve = POOL_CH * PHASES, DVE_CH * PHASES
    loads = [PHASES] * RG
    free_at = [("pool", pool - 2), ("pool", pool), ("dve", dve)]
    used0 = CH * PHASES

    def group(what, k, width, slots, used):
        nonlocal pool, dve
        g = group.n % RG
        group.n += 1
        loads[g] += 1
        free = free_at[g]
        for m, (slot, need) in enumerate(zip(slots, used)):
            who = "dve" if g == RG - 1 else "pool"
            if who == "dve":
                dve += 1
            else:
                pool += 1
            plan.append(dict(what=what, k=k + m, width=width, raw_group=g, raw_at=m * width,
                             first=m == 0, chunks=len(slots), free=free, full=16 * loads[g],
                             ring_at=slot * width, used=need, who=who,
                             lo=dve if who == "dve" else pool, n=used0 + len(plan)))
        free_at[g] = (who, dve if who == "dve" else pool)

    group.n = 0
    views = CH * D // HC
    for i in range(2 * KD):
        if i < views:
            last = (HC * (i + 1) - 1) // D
            need = used0 - CH + last + 1
        else:
            need = used0 + i - views + 1
        group("W1" if i < KD else "Wr1", i % KD, HC, [i % views], [need])
    wide = 2 * KD
    for i in range(0, 2 * KH, 2):
        slots, needs = [], []
        for j in (i, i + 1):
            slots.append(j % CH)
            if j < CH:
                last = min((D * (j + 1) - 1) // HC, views - 1)
                needs.append(used0 + wide - views + last + 1)
            else:
                needs.append(used0 + wide + j - CH + 1)
        group("W2" if i < KH else "Wr2", i % KH, D, slots, needs)
    return plan


def build_gnn(nc, x, src, dst, b0_W1, b0_as1, b0_ad1, b0_b1, b0_W2, b0_as2, b0_ad2, b0_b2,
              b1_W1, b1_as1, b1_ad1, b1_b1, b1_g1, b1_be1, b1_Wr1, b1_br1,
              b1_W2, b1_as2, b1_ad2, b1_b2, b1_g2, b1_be2, b1_Wr2, b1_br2, out):
    plan = block1_plan()
    wide_chunks = 2 * KD
    ctx = ExitStack()
    with ctx:
        def sb(name, shape, dt=F32):
            return ctx.enter_context(nc.sbuf_tensor(name, shape, dt))

        def sem(name):
            return ctx.enter_context(nc.semaphore(name))

        x_sb = sb("x_sb", [P, NT, D])
        xT_hi = sb("xT_hi", [P, KD, N], F32R)
        xT_lo = sb("xT_lo", [P, KD, N], F32R)
        counts = sb("counts", [P, NT, N])
        far = sb("far", [P, NT, N])
        ident = sb("ident", [P, P])
        ones = sb("ones", [P, P])
        zeros = sb("zeros", [P, P], BF16)
        iota = sb("iota", [P, N], BF16)
        edges = sb("edges", [P, 2, ET], I32)
        edges_f = sb("edges_f", [P, 2, ET])
        raw = sb("raw", [P, RG, 2 * D])
        ring_hi = sb("ring_hi", [P, CH * D], F32R)
        ring_lo = sb("ring_lo", [P, CH * D], F32R)
        att = sb("att", [P, 2 * HC])
        hs = sb("hs", [P, NT * HC])
        h_hi = sb("h_hi", [P, NT * HC], F32R)
        h_lo = sb("h_lo", [P, NT * HC], F32R)
        pT_hi = sb("pT_hi", [P, H1, NT, N], F32R)
        pT_lo = sb("pT_lo", [P, H1, NT, N], F32R)
        zT_hi = sb("zT_hi", [P, KH, N], F32R)
        zT_lo = sb("zT_lo", [P, KH, N], F32R)
        z = sb("z", [P, KH * N])
        am = sb("am", [P, H1, NT, N])
        e1 = sb("e1", [P, H1, NT, N])
        e2 = sb("e2", [P, H1, NT, N])
        diag = sb("diag", [P, H1, N])
        b1_cols = sb("b1_cols", [P, H0 * KD])
        b1_rows = sb("b1_rows", [H0 * KD, P])
        rows_hc = sb("rows_hc", [P, 4, HC])
        rows_d = sb("rows_d", [P, 4, D])
        S = 2 * H1
        a_s = sb("a_s", [P, S])
        a_d = sb("a_d", [P, S])
        a_d2 = sb("a_d2", [P, S])
        mx = sb("mx", [P, S])
        zc = sb("zc", [P, S])
        mm = sb("mm", [P, S])
        bias1 = sb("bias1", [P, S])
        bias2 = sb("bias2", [P, S])
        zsum = sb("zsum", [P, S])
        rz = sb("rz", [P, S])
        stats = sb("stats", [P, NT, 2, 6])
        mv = sb("mv", [P, NT, 2])
        ve = sb("ve", [P, NT])
        rstd = sb("rstd", [P, NT])
        half = sb("half", [P, 1])

        hot_homes = [t.bitcast(BF16) for t in (am[:].rearrange("p a b c -> p (a b c)"),
                                               e1[:].rearrange("p a b c -> p (a b c)"),
                                               e2[:].rearrange("p a b c -> p (a b c)"), z[:])]
        per_home = ET // len(hot_homes)

        def hot(t, which):
            at = ((t % per_home) * 2 + which) * N
            return hot_homes[t // per_home][:, at:at + N]

        iota_i = hs[:, 0:N].bitcast(I32)

        ps = ctx.enter_context(nc.psum_tensor("ps", [P, 8 * BANK], F32))
        PROJ, ACC = 0, 3 * BANK
        S_AT, T_AT = 6 * BANK, 7 * BANK
        NAT_AT = [0, 6 * BANK]
        ELU_AT = [2 * BANK, 6 * BANK, 7 * BANK]

        raw_full = [sem(f"raw_full{g}") for g in range(RG)]
        hi_done = sem("hi_done")
        lo_by = {"pool": sem("lo_pool"), "dve": sem("lo_dve")}
        chunk_used = sem("chunk_used")
        x_loaded = sem("x_loaded")
        b2_loaded = sem("b2_loaded")
        edges_loaded = sem("edges_loaded")
        b1_loaded = sem("b1_loaded")
        rows_loaded = sem("rows_loaded")
        att_loaded = sem("att_loaded")
        consts = sem("consts")
        iota_ready = sem("iota_ready")
        xT_ps = sem("xT_ps")
        xT_hi_done = sem("xT_hi_done")
        xT_lo_done = sem("xT_lo_done")
        edges_cast = sem("edges_cast")
        hot_done = sem("hot_done")
        counted = sem("counted")
        counts_copied = sem("counts_copied")
        counts_done = sem("counts_done")
        far_done = sem("far_done")
        b1_ps = sem("b1_ps")
        b1_ready = sem("b1_ready")
        xb_done = sem("xb_done")
        hs_done = sem("hs_done")
        h_hi_done = sem("h_hi_done")
        h_lo_done = sem("h_lo_done")
        a_src_done = sem("a_src_done")
        a_dst_done = sem("a_dst_done")
        diag_done = sem("diag_done")
        scores_bc = sem("scores_bc")
        slope_done = sem("slope_done")
        masked = sem("masked")
        top_done = sem("top_done")
        m_done = sem("m_done")
        bias_done = sem("bias_done")
        exps_done = sem("exps_done")
        emax_done = sem("emax_done")
        p_done = sem("p_done")
        rz_done = sem("rz_done")
        norm_done = sem("norm_done")
        pT_ps = sem("pT_ps")
        pT_hi_done = sem("pT_hi_done")
        pT_lo_done = sem("pT_lo_done")
        agg_done = sem("agg_done")
        elu_exp = sem("elu_exp")
        elu_neg = sem("elu_neg")
        z_done = sem("z_done")
        z_hi_done = sem("z_hi_done")
        z_lo_done = sem("z_lo_done")
        nat_done = sem("nat_done")
        biased = sem("biased")
        stats_done = sem("stats_done")
        aggr_done = sem("aggr_done")
        ve_done = sem("ve_done")
        rstd_done = sem("rstd_done")
        norm1 = sem("norm1")
        norm2 = sem("norm2")
        x1_done = sem("x1_done")
        x1T_ps = sem("x1T_ps")
        x1T_hi_done = sem("x1T_hi_done")
        x1T_lo_done = sem("x1T_lo_done")
        r_done = sem("r_done")
        r_added = sem("r_added")
        h1_done = sem("h1_done")
        h1T_ps = sem("h1T_ps")
        h1T_hi_done = sem("h1T_hi_done")
        h1T_lo_done = sem("h1T_lo_done")
        r2_done = sem("r2_done")
        r2_added = sem("r2_added")
        summed = sem("summed")
        out_ready = sem("out_ready")
        stored = sem("stored")

        block = ctx.enter_context(nc.Block())

        def slot_hi(c):
            return ring_hi[:, c * D:(c + 1) * D]

        def slot_lo(c):
            return ring_lo[:, c * D:(c + 1) * D]

        def raw_chunk(c):
            return raw[:, c // 2, (c % 2) * D:(c % 2 + 1) * D]

        def split_hi(eng, p, c, reused=True):
            if c % 2 == 0:
                eng.wait_ge(raw_full[c // 2], 16 * p + 16)
            if reused:
                eng.wait_ge(chunk_used, CH * p + c - CH + 1)
            eng.activation(slot_hi(c), raw_chunk(c), ACT.Copy).then_inc(hi_done, 1)

        def split_lo(eng, p, c):
            eng.wait_ge(hi_done, CH * p + c + 1)
            eng.tensor_tensor(slot_lo(c), raw_chunk(c), slot_hi(c).bitcast(F32), ALU.subtract)\
               .then_inc(lo_by["pool" if c < POOL_CH else "dve"], 1)

        def split_hi1(eng, q):
            if q["first"]:
                eng.wait_ge(raw_full[q["raw_group"]], q["full"])
            eng.wait_ge(chunk_used, q["used"])
            w = q["width"]
            eng.activation(ring_hi[:, q["ring_at"]:q["ring_at"] + w],
                           raw[:, q["raw_group"], q["raw_at"]:q["raw_at"] + w], ACT.Copy)\
               .then_inc(hi_done, 1)

        def split_lo1(eng, q):
            eng.wait_ge(hi_done, q["n"] + 1)
            w = q["width"]
            eng.tensor_tensor(ring_lo[:, q["ring_at"]:q["ring_at"] + w],
                              raw[:, q["raw_group"], q["raw_at"]:q["raw_at"] + w],
                              ring_hi[:, q["ring_at"]:q["ring_at"] + w].bitcast(F32), ALU.subtract)\
               .then_inc(lo_by[q["who"]], 1)

        def is_gat1(a):
            return isinstance(a, int) and a == A_GAT1

        def heads_of(a):
            return H1 if is_gat1(a) else 1

        def feat(t, a, i):
            w = HC if is_gat1(a) else D
            return t[:, i * w:(i + 1) * w]

        def source_of(a):
            return ACC if isinstance(a, int) and a == A_CONV2 else PROJ

        def pT_at(a, k):
            return [2, 3, 0, 1][k] * BANK if is_gat1(a) else T_AT

        def s_at(a, k):
            return k * N if is_gat1(a) else S_AT

        def before(a):
            return 2 * a if not isinstance(a, int) or a <= A_GAT1 else 2 * (A_GAT1 + H1) + 2 * (a - A_GAT1 - 1)

        def heads_before(a):
            return a if not isinstance(a, int) or a <= A_GAT1 else A_GAT1 + H1 + (a - A_GAT1 - 1)

        PASSES = 3

        def three(hi_a, lo_a, hi_b, lo_b):
            return ((hi_a, hi_b), (hi_a, lo_b), (lo_a, hi_b))

        @block.sync
        def _(sp):
            w1 = b0_W1.rearrange("(k p) (h c) -> p k h c", p=P, c=D)
            w2 = b0_W2.rearrange("(h k p) c -> p h k c", p=P, k=KD)

            def load(p, g, view):
                dst_ap = raw[:, g, :].rearrange("p (k c) -> p k c", k=2)
                sp.dma_start(dst_ap, view).then_inc(raw_full[g], 16)

            def load_phase(p, view, reused=True):
                for g in range(RG):
                    if reused:
                        if g < RG - 1:
                            sp.wait_ge(lo_by["pool"], POOL_CH * p - POOL_CH + 2 * (g + 1))
                        else:
                            sp.wait_ge(lo_by["dve"], DVE_CH * p)
                    load(p, g, view(g))

            def w1_of(h):
                return lambda g: w1[:, 2 * g:2 * g + 2, bass.ds(h, 1), :].rearrange("p k h c -> p k (h c)")

            def w2_of(h):
                return lambda g: w2[:, bass.ds(h, 1), 2 * g:2 * g + 2, :].rearrange("p h k c -> p (h k) c")

            sp.dma_start(x_sb[:, :, :], x.rearrange("(t p) c -> p t c", p=P)).then_inc(x_loaded, 16)
            load_phase(0, w1_of(0), reused=False)
            load_phase(1, w1_of(1))
            load_phase(2, w2_of(0))
            with sp.Fori(2, H0) as h:
                load_phase(2 * h - 1, w1_of(h))
                load_phase(2 * h, w2_of(h - 1))
            load_phase(PHASES - 1, w2_of(H0 - 1))
            views = {"W1": b1_W1, "Wr1": b1_Wr1, "W2": b1_W2, "Wr2": b1_Wr2}
            for q in plan:
                if not q["first"]:
                    continue
                who, count = q["free"]
                sp.wait_ge(lo_by[who], count)
                view = views[q["what"]].rearrange("(k p) c -> p k c", p=P)[:, q["k"]:q["k"] + q["chunks"], :]
                width = q["chunks"] * q["width"]
                sp.dma_start(raw[:, q["raw_group"], 0:width].rearrange("p (k c) -> p k c", k=q["chunks"]),
                             view).then_inc(raw_full[q["raw_group"]], 16)
            for i in range(NT):
                sp.wait_ge(out_ready, i + 1)
                sp.dma_start(out[i * P:(i + 1) * P, :], x_sb[:, i, :]).then_inc(stored, 16)
            sp.wait_ge(stored, 16 * NT)

        @block.gpsimd
        def _(pool):
            pool.memset(ident[:, :], 0.0).then_inc(consts, 1)
            pool.wait_ge(consts, 1)
            pool.affine_select(out=ident[:, :], in_=ident[:, :], compare_op=ALU.not_equal, fill=1.0,
                               base=0, pattern=[[-1, P]], channel_multiplier=1).then_inc(consts, 1)
            pool.iota(iota_i, pattern=[[1, N]], base=0, channel_multiplier=0).then_inc(iota_ready, 1)
            pool.memset(ones[:, :], 1.0).then_inc(consts, 1)
            pool.memset(zeros[:, :], 0.0).then_inc(consts, 1)
            pool.memset(half[:, :], -0.5).then_inc(consts, 1)
            for c in range(POOL_CH):
                split_lo(pool, 0, c)

            def features_lo(a):
                for i in range(NT):
                    pool.wait_ge(h_hi_done, 2 * a + i + 1)
                    pool.tensor_tensor(feat(h_lo, a, i), feat(hs, a, i), feat(h_hi, a, i).bitcast(F32),
                                       ALU.subtract).then_inc(h_lo_done, 1)

            def head(h, first=False):
                if not first:
                    for c in range(POOL_CH):
                        split_lo(pool, 2 * h, c)
                features_lo(h)
                for c in range(POOL_CH):
                    split_lo(pool, 2 * h + 1, c)

            head(0, first=True)
            pool.wait_ge(b2_loaded, 16)
            pool.wait_ge(xT_ps, 3)
            for i in range(NT):
                pool.tensor_tensor(x_sb[:, i, :], x_sb[:, i, :], rows_d[:, 3, :], ALU.add).then_inc(xb_done, 1)
            with pool.Fori(1, H0) as h:
                head(h)

            def inverse_root(n, i):
                pool.wait_ge(ve_done, NT * n + i + 1)
                pool.tensor_tensor(rstd[:, i:i + 1], ve[:, i:i + 1], half[:, :], ALU.pow).then_inc(rstd_done, 1)

            mine = [q for q in plan if q["who"] == "pool"]
            wide = [q for q in mine if q["width"] == HC]
            narrow = [q for q in mine if q["width"] == D]
            features_lo(A_CONV2)
            for q in wide[:3]:
                split_lo1(pool, q)
            for i in range(NT):
                inverse_root(0, i)
            for q in wide[3:6]:
                split_lo1(pool, q)
            features_lo(A_GAT1)
            for q in wide[6:]:
                split_lo1(pool, q)
            for q in narrow[:4]:
                split_lo1(pool, q)
            for i in range(NT):
                inverse_root(1, i)
            for q in narrow[4:8]:
                split_lo1(pool, q)
            features_lo(A_GAT2)
            for q in narrow[8:]:
                split_lo1(pool, q)
            for n in (2, 3):
                for i in range(NT):
                    inverse_root(n, i)

        @block.scalar
        def _(act):
            def load_att(n, a_src, a_dst, width, reused=True):
                if reused:
                    act.wait_ge(a_dst_done, 2 * n)
                for half_at, v in ((0, a_src), (1, a_dst)):
                    act.dma_start(att[:, half_at * width:(half_at + 1) * width], v.partition_broadcast(P))\
                       .then_inc(att_loaded, 16)

            def att_row(t, h):
                return t[bass.ds(h, 1), :]

            act.dma_start(edges[:, 0, :], src.rearrange("(p t) -> p t", p=P)).then_inc(edges_loaded, 16)
            act.dma_start(edges[:, 1, :], dst.rearrange("(p t) -> p t", p=P)).then_inc(edges_loaded, 16)
            act.dma_start(b1_rows[:, :], b0_b1.rearrange("(t p) -> t p", p=P)).then_inc(b1_loaded, 16)
            load_att(0, b0_as1[0:1, :], b0_ad1[0:1, :], D, reused=False)

            for b in range(3):
                act.wait_ge(xT_ps, b + 1)
                act.activation(xT_hi[:, 2 * b:2 * b + 2, :].rearrange("p k n -> p (k n)"),
                               ps[:, (5 + b) * BANK:(6 + b) * BANK], ACT.Copy).then_inc(xT_hi_done, 1)
            for c in range(CH):
                split_hi(act, 0, c, reused=False)
            act.dma_start(rows_d[:, 3, :], b0_b2.partition_broadcast(P)).then_inc(b2_loaded, 16)
            for n, v in enumerate((b1_b1, b1_g1, b1_be1, b1_br1)):
                act.dma_start(rows_hc[:, n, :], v.partition_broadcast(P)).then_inc(rows_loaded, 16)
            for n, v in enumerate((b1_b2, b1_g2, b1_be2)):
                act.dma_start(rows_d[:, n, :], v.partition_broadcast(P)).then_inc(rows_loaded, 16)

            def features(a, chunks):
                at = source_of(a)
                w = HC if is_gat1(a) else D
                act.wait_ge(chunk_used, chunks)
                for i in range(NT):
                    act.activation(feat(hs, a, i), ps[:, at + i * w:at + (i + 1) * w], ACT.Copy)\
                       .then_inc(hs_done, 1)
                for i in range(NT):
                    act.wait_ge(hs_done, 2 * a + i + 1)
                    act.activation(feat(h_hi, a, i), feat(hs, a, i), ACT.Copy).then_inc(h_hi_done, 1)

            def exps(a):
                for k in range(heads_of(a)):
                    if k == 0:
                        act.wait_ge(bias_done, 2 * a + 2)
                    for i in range(NT):
                        c = 2 * k + i
                        act.activation(e1[:, k, i, :], am[:, k, i, :], ACT.Exp, bias=bias1[:, c:c + 1])\
                           .then_inc(exps_done, 1)
                        act.activation(e2[:, k, i, :], am[:, k, i, :], ACT.Exp, bias=bias2[:, c:c + 1],
                                       scale=SLOPE).then_inc(exps_done, 1)

            def weights_hi(a):
                for k in range(heads_of(a)):
                    act.wait_ge(pT_ps, heads_before(a) + k + 1)
                    at = pT_at(a, k)
                    act.activation(pT_hi[:, k, :, :].rearrange("p j n -> p (j n)"), ps[:, at:at + 2 * N],
                                   ACT.Copy).then_inc(pT_hi_done, 1)

            def elu(h, first=False):
                for q in range(3):
                    act.wait_ge(agg_done, 3 * h + q + 1)
                    if not first:
                        act.wait_ge(z_lo_done, 3 * h + q - 2)
                    for c in range(2):
                        t = 2 * q + c
                        act.activation(z[:, t * N:(t + 1) * N], ps[:, ELU_AT[q] + c * N:ELU_AT[q] + (c + 1) * N],
                                       ACT.Exp, bias=b1_cols[:, bass.ds(KD * h + t, 1)]).then_inc(elu_exp, 1)
                    if q >= 1:
                        elu_hi(h, q - 1)
                elu_hi(h, 2)

            def elu_hi(h, q):
                act.wait_ge(z_done, 6 * h + 2 * q + 2)
                act.activation(zT_hi[:, 2 * q:2 * q + 2, :].rearrange("p k n -> p (k n)"),
                               z[:, 2 * q * N:(2 * q + 2) * N], ACT.Copy).then_inc(z_hi_done, 1)

            def head(h, first=False, last=False):
                if not first:
                    for c in range(CH):
                        split_hi(act, 2 * h, c)
                features(h, CH if first else 2 * CH * h)
                for c in (0, 1):
                    split_hi(act, 2 * h + 1, c)
                if last:
                    load_att(h + 1, b0_as2[0:1, :], b0_ad2[0:1, :], D)
                else:
                    load_att(h + 1, att_row(b0_as1, h + 1), att_row(b0_ad1, h + 1), D)
                exps(h)
                for c in (2, 3):
                    split_hi(act, 2 * h + 1, c)
                weights_hi(h)
                for c in (4, 5):
                    split_hi(act, 2 * h + 1, c)
                if first:
                    act.wait_ge(b1_ready, 1)
                elu(h, first)

            head(0, first=True)
            with act.Fori(1, H0 - 1) as h:
                head(h)
            head(H0 - 1, last=True)

            act.wait_ge(xb_done, NT)
            act.dma_start(rows_d[:, 3, :], b1_br2.partition_broadcast(P)).then_inc(rows_loaded, 16)

            features(A_CONV2, CH * PHASES)
            load_att(A_GAT1, b1_as1.rearrange("h c -> (h c)"), b1_ad1.rearrange("h c -> (h c)"), HC)
            split_hi1(act, plan[0])
            exps(A_CONV2)
            split_hi1(act, plan[1])
            weights_hi(A_CONV2)
            split_hi1(act, plan[2])
            split_hi1(act, plan[3])
            for i in range(NT):
                act.wait_ge(x1T_ps, i + 1)
                at = ACC + 2 * i * BANK
                act.activation(xT_hi[:, :, i * P:(i + 1) * P],
                               ps[:, at:at + D].rearrange("p (k n) -> p k n", n=P), ACT.Copy)\
                   .then_inc(x1T_hi_done, 1)
            for q in plan[4:8]:
                split_hi1(act, q)
            features(A_GAT1, plan[KD - 1]["n"] + 1)
            for q in plan[8:10]:
                split_hi1(act, q)
            exps(A_GAT1)
            act.wait_ge(a_dst_done, before(A_GAT1) + 2 * H1)
            for half_at, v in ((0, b1_as2), (1, b1_ad2)):
                act.dma_start(att[:, half_at * D:(half_at + 1) * D], v[0:1, :].partition_broadcast(P))\
                   .then_inc(att_loaded, 16)
            for q in plan[10:12]:
                split_hi1(act, q)
            weights_hi(A_GAT1)
            for q in plan[12:18]:
                split_hi1(act, q)
            for i in range(NT):
                act.wait_ge(h1T_ps, i + 1)
                at = 4 * BANK + i * HC
                act.activation(zT_hi[:, :, i * P:(i + 1) * P],
                               ps[:, at:at + HC].rearrange("p (k n) -> p k n", n=P), ACT.Copy)\
                   .then_inc(h1T_hi_done, 1)
            for q in plan[18:22]:
                split_hi1(act, q)
            features(A_GAT2, plan[2 * KD + KH - 1]["n"] + 1)
            for q in plan[22:24]:
                split_hi1(act, q)
            exps(A_GAT2)
            for q in plan[24:26]:
                split_hi1(act, q)
            weights_hi(A_GAT2)
            for q in plan[26:]:
                split_hi1(act, q)

        @block.tensor
        def _(pe):
            def pieces(i):
                return ((0, BANK, 0), (BANK, D, BANK)) if i == 0 else ((0, N, D), (N, D, 2 * BANK))

            def product(at, i, lhs_hi, lhs_lo, w_hi, w_lo, start, stop, bank2_wait=None):
                last = None
                for n, (a, b) in enumerate(three(lhs_hi, lhs_lo, w_hi, w_lo)):
                    for lo, hi, to in pieces(i):
                        if to == 2 * BANK and n == 0 and bank2_wait is not None:
                            pe.wait_ge(*bank2_wait)
                        last = pe.matmul(ps[:, at + to:at + to + hi - lo], a, b[:, lo:hi],
                                         start=start and n == 0 and to != D,
                                         stop=stop and n == PASSES - 1, skip_group_check=True)
                return last

            def chunk(p, c):
                if c < POOL_CH:
                    pe.wait_ge(lo_by["pool"], POOL_CH * p + c + 1)
                else:
                    pe.wait_ge(lo_by["dve"], DVE_CH * p + c - POOL_CH + 1)

            def node_tile(t, k, i):
                return t[:, k, i * P:(i + 1) * P]

            def project(p, h, first=False):
                for c in range(CH):
                    chunk(p, c)
                    if first and c % 2 == 0:
                        pe.wait_ge(xT_lo_done, c // 2 + 1)
                    for i in range(NT):
                        wait = (z_done, 6 * h - 4) if c == 0 and i == 1 and not first else None
                        last = product(PROJ, i, node_tile(xT_hi, c, i), node_tile(xT_lo, c, i),
                                       slot_hi(c), slot_lo(c), c == 0, c == CH - 1, wait)
                    last.then_inc(chunk_used, 1)

            def accumulate(p, h, c, last_head=False):
                if c % 2 == 0:
                    pe.wait_ge(z_lo_done, 3 * h + c // 2 + 1)
                chunk(p, c)
                for i in range(NT):
                    last = product(ACC, i, node_tile(zT_hi, c, i), node_tile(zT_lo, c, i),
                                   slot_hi(c), slot_lo(c), False, last_head and c == CH - 1)
                last.then_inc(chunk_used, 1)

            def scores(a):
                pe.wait_ge(diag_done, before(a) + 2 * heads_of(a))
                n = heads_of(a)
                for k in range(0, n, 2):
                    m = min(2, n - k)
                    last = pe.matmul(ps[:, s_at(a, k):s_at(a, k) + m * N], ones[:, :],
                                     diag[:, k:k + m, :].rearrange("p k n -> p (k n)"), start=True, stop=True)
                last.then_inc(scores_bc, 1)

            def weights(a):
                for k in range(heads_of(a)):
                    pe.wait_ge(norm_done, before(a) + 2 * (k + 1))
                    for j in range(NT):
                        for i in range(NT):
                            at = pT_at(a, k) + j * N + i * P
                            last = pe.matmul(ps[:, at:at + P], am[:, k, i, j * P:(j + 1) * P],
                                             diag[:, k, i * P:(i + 1) * P], start=True, stop=True)
                    last.then_inc(pT_ps, 1)

            def aggregate_T(h):
                pe.wait_ge(h_lo_done, 2 * h + 2)
                pe.wait_ge(pT_lo_done, h + 1)
                for q in range(3):
                    for c in range(2):
                        ch = (2 * q + c) * P
                        for j in range(NT):
                            f = [feat(t, 0, j)[:, ch:ch + P] for t in (h_hi, h_lo)]
                            for n, (a, b) in enumerate(three(*f, pT_hi[:, 0, j, :], pT_lo[:, 0, j, :])):
                                last = pe.matmul(ps[:, ELU_AT[q] + c * N:ELU_AT[q] + (c + 1) * N], a, b,
                                                 start=c == 0 and j == 0 and n == 0,
                                                 stop=j == NT - 1 and n == PASSES - 1, skip_group_check=True)
                    last.then_inc(agg_done, 1)

            def aggregate(a):
                pe.wait_ge(h_lo_done, 2 * a + 2)
                pe.wait_ge(pT_lo_done, heads_before(a) + 1)
                for i in range(NT):
                    for j in range(NT):
                        w = [t[:, 0, j, i * P:(i + 1) * P] for t in (pT_hi, pT_lo)]
                        for n, (l, r) in enumerate(three(*w, feat(h_hi, a, j), feat(h_lo, a, j))):
                            for lo, hi in ((0, BANK), (BANK, D)):
                                last = pe.matmul(ps[:, NAT_AT[i] + lo:NAT_AT[i] + hi], l, r[:, lo:hi],
                                                 start=j == 0 and n == 0, stop=j == NT - 1 and n == PASSES - 1)
                    last.then_inc(nat_done, 1)

            pe.wait_ge(consts, 5)
            pe.wait_ge(x_loaded, 16)
            for b in range(3):
                for k in (2 * b, 2 * b + 1):
                    for i in range(NT):
                        at = 5 * BANK + k * N + i * P
                        last = pe.transpose(ps[:, at:at + P], x_sb[:, i, k * P:(k + 1) * P], ident[:, :])
                last.then_inc(xT_ps, 1)
            pe.wait_ge(b1_loaded, 16)
            pe.transpose(ps[:, 3 * BANK:3 * BANK + H0 * KD], b1_rows[:, :], ident[0:H0 * KD, 0:H0 * KD])\
              .then_inc(b1_ps, 1)
            project(0, 0, first=True)
            pe.wait_ge(xT_lo_done, 3)
            for i in range(NT):
                for t in range(ET):
                    if i == 0 and t % per_home == 0:
                        pe.wait_ge(hot_done, 2 * (t + per_home))
                    last = pe.matmul(ps[:, (6 + i) * BANK:(6 + i) * BANK + N], hot(t, 1)[:, i * P:(i + 1) * P],
                                     hot(t, 0), start=t == 0, stop=t == ET - 1)
                last.then_inc(counted, 1)
            pe.wait_ge(b1_ready, 1)
            for b in range(3):
                for part in range(2):
                    at = ACC + b * BANK + part * N
                    pe.matmul(ps[:, at:at + N], zeros[:, :], iota[:, :], start=part == 0, stop=False,
                              skip_group_check=True)
            pe.wait_ge(counts_copied, 2)
            scores(0)
            weights(0)
            aggregate_T(0)

            def head(h):
                project(2 * h - 1, h)
                for c in range(CH):
                    if c == 2:
                        pe.wait_ge(z_done, 6 * h)
                        scores(h)
                    if c == 5:
                        weights(h)
                    accumulate(2 * h, h - 1, c)
                aggregate_T(h)

            with pe.Fori(1, H0) as h:
                head(h)
            for c in range(CH):
                accumulate(PHASES - 1, H0 - 1, c, last_head=True)

            pe.wait_ge(z_done, 6 * H0)
            scores(A_CONV2)
            weights(A_CONV2)
            aggregate(A_CONV2)
            for i in range(NT):
                pe.wait_ge(x1_done, i + 1)
                for k in range(KD):
                    at = ACC + 2 * i * BANK + k * P
                    last = pe.transpose(ps[:, at:at + P], x_sb[:, i, k * P:(k + 1) * P], ident[:, :])
                last.then_inc(x1T_ps, 1)

            def wide_product(q, at):
                pe.wait_ge(lo_by[q["who"]], q["lo"])
                k, w = q["k"], q["ring_at"]
                for i in range(NT):
                    for n, (a, b) in enumerate(three(node_tile(xT_hi, k, i), node_tile(xT_lo, k, i),
                                                     ring_hi[:, w:w + HC], ring_lo[:, w:w + HC])):
                        for part in range(2):
                            to = at + i * HC + part * BANK
                            last = pe.matmul(ps[:, to:to + BANK], a, b[:, part * BANK:(part + 1) * BANK],
                                             start=k == 0 and n == 0, stop=k == KD - 1 and n == PASSES - 1)
                last.then_inc(chunk_used, 1)

            def narrow_product(q, at):
                pe.wait_ge(lo_by[q["who"]], q["lo"])
                k, w = q["k"], q["ring_at"]
                for i in range(NT):
                    last = product(at, i, node_tile(zT_hi, k, i), node_tile(zT_lo, k, i),
                                   ring_hi[:, w:w + D], ring_lo[:, w:w + D], k == 0, k == KH - 1)
                last.then_inc(chunk_used, 1)

            pe.wait_ge(x1T_lo_done, NT)
            for q in plan[:KD]:
                wide_product(q, 0)
            for q in plan[KD:2 * KD]:
                if q["k"] == 3:
                    scores(A_GAT1)
                wide_product(q, 4 * BANK)
            weights(A_GAT1)
            pe.wait_ge(h_lo_done, 2 * A_GAT1 + 2)
            pe.wait_ge(pT_lo_done, heads_before(A_GAT1) + H1)
            for i in range(NT):
                for k in range(H1):
                    for j in range(NT):
                        f = [feat(t, A_GAT1, j)[:, k * C1:(k + 1) * C1] for t in (h_hi, h_lo)]
                        w = [t[:, k, j, i * P:(i + 1) * P] for t in (pT_hi, pT_lo)]
                        for n, (a, b) in enumerate(three(*w, *f)):
                            to = i * HC + k * C1
                            last = pe.matmul(ps[:, to:to + C1], a, b, start=k % 2 == 0 and j == 0 and n == 0,
                                             stop=j == NT - 1 and n == PASSES - 1, skip_group_check=True)
                last.then_inc(nat_done, 1)
            for i in range(NT):
                pe.wait_ge(h1_done, i + 1)
                for k in range(KH):
                    at = 4 * BANK + i * HC + k * P
                    last = pe.transpose(ps[:, at:at + P], z[:, i * HC + k * P:i * HC + (k + 1) * P], ident[:, :])
                last.then_inc(h1T_ps, 1)
            pe.wait_ge(h1T_lo_done, NT)
            for q in plan[2 * KD:2 * KD + KH]:
                narrow_product(q, 0)
            for q in plan[2 * KD + KH:]:
                if q["k"] == 2:
                    scores(A_GAT2)
                if q["k"] == 6:
                    weights(A_GAT2)
                narrow_product(q, 3 * BANK)
            aggregate(A_GAT2)

        @block.vector
        def _(dve):
            def input_lo(b):
                dve.wait_ge(xT_hi_done, b + 1)
                dve.tensor_tensor(xT_lo[:, 2 * b:2 * b + 2, :].rearrange("p k n -> p (k n)"),
                                  ps[:, (5 + b) * BANK:(6 + b) * BANK],
                                  xT_hi[:, 2 * b:2 * b + 2, :].rearrange("p k n -> p (k n)").bitcast(F32),
                                  ALU.subtract).then_inc(xT_lo_done, 1)

            dve.wait_ge(edges_loaded, 32)
            dve.wait_ge(iota_ready, 1)
            dve.tensor_copy(iota[:, :], iota_i).then_inc(edges_cast, 1)
            dve.tensor_copy(edges_f[:, :, :], edges[:, :, :]).then_inc(edges_cast, 1)
            for b in range(3):
                input_lo(b)
            dve.wait_ge(b1_ps, 1)
            dve.tensor_copy(b1_cols[:, :], ps[:, 3 * BANK:3 * BANK + H0 * KD]).then_inc(b1_ready, 1)
            for c in range(POOL_CH, CH):
                split_lo(dve, 0, c)
            dve.wait_ge(edges_cast, 2)
            for t in range(ET):
                for which in range(2):
                    dve.tensor_scalar(hot(t, which), iota[:, :], edges_f[:, which, t:t + 1], None,
                                      ALU.is_equal).then_inc(hot_done, 1)

            def dots(a, t, half_at, done):
                n = heads_of(a)
                w = C1 if n > 1 else D
                for i in range(NT):
                    if half_at == 0:
                        dve.wait_ge(hs_done, 2 * a + i + 1)
                    for k in range(n):
                        junk = (e1, e2)[half_at][:].rearrange("p a b c -> p (a b c)")
                        at = (i * n + k) * w
                        dve.tensor_tensor_reduce(junk[:, at:at + w], feat(hs, a, i)[:, k * w:(k + 1) * w],
                                                 att[:, (half_at * n + k) * w:(half_at * n + k + 1) * w],
                                                 1.0, 0.0, ALU.mult, ALU.add, t[:, 2 * k + i:2 * k + i + 1])\
                           .then_inc(done, 1)

            def attention(a):
                n = heads_of(a)
                upto = before(a) + 2 * n
                small = slice(0, 2 * n)
                dve.wait_ge(att_loaded, 32 * a + 32)
                dots(a, a_s, 0, a_src_done)
                dve.wait_ge(a_src_done, upto)
                for k in range(n):
                    for i in range(NT):
                        dve.tensor_scalar(diag[:, k, i * P:(i + 1) * P], ident[:, :],
                                          a_s[:, 2 * k + i:2 * k + i + 1], None, ALU.mult).then_inc(diag_done, 1)
                dots(a, a_d, 1, a_dst_done)
                dve.wait_ge(a_dst_done, upto)
                dve.wait_ge(scores_bc, a + 1)
                dve.tensor_scalar(a_d2[:, small], a_d[:, small], SLOPE, None, ALU.mult).then_inc(slope_done, 1)
                for k in range(n):
                    for i in range(NT):
                        dve.tensor_tensor_reduce(am[:, k, i, :], ps[:, s_at(a, k):s_at(a, k) + N], far[:, i, :],
                                                 1.0, -3.0e38, ALU.add, ALU.max, mx[:, 2 * k + i:2 * k + i + 1])\
                           .then_inc(masked, 1)
                dve.wait_ge(masked, upto)
                dve.tensor_tensor(zc[:, small], mx[:, small], a_d[:, small], ALU.add).then_inc(top_done, 1)
                dve.wait_ge(top_done, a + 1)
                dve.scalar_tensor_tensor(mm[:, small], zc[:, small], SLOPE, zc[:, small], ALU.mult, ALU.max)\
                   .then_inc(m_done, 1)
                dve.wait_ge(m_done, a + 1)
                dve.tensor_tensor(bias1[:, small], a_d[:, small], mm[:, small], ALU.subtract).then_inc(bias_done, 1)
                dve.tensor_tensor(bias2[:, small], a_d2[:, small], mm[:, small], ALU.subtract).then_inc(bias_done, 1)
                for k in range(n):
                    dve.wait_ge(exps_done, 2 * before(a) + 4 * (k + 1))
                    dve.tensor_tensor(e1[:, k, :, :], e1[:, k, :, :], e2[:, k, :, :], ALU.max)\
                       .then_inc(emax_done, 1)
                    dve.wait_ge(emax_done, heads_before(a) + k + 1)
                    for i in range(NT):
                        c = 2 * k + i
                        dve.scalar_tensor_tensor(am[:, k, i, :], e1[:, k, i, :], 1.0, counts[:, i, :], ALU.mult,
                                                 ALU.mult, accum_out=zsum[:, c:c + 1]).then_inc(p_done, 1)
                    dve.wait_ge(p_done, before(a) + 2 * (k + 1))
                    dve.reciprocal(rz[:, 2 * k:2 * k + 2], zsum[:, 2 * k:2 * k + 2]).then_inc(rz_done, 1)
                    dve.wait_ge(rz_done, heads_before(a) + k + 1)
                    for i in range(NT):
                        c = 2 * k + i
                        dve.tensor_scalar(diag[:, k, i * P:(i + 1) * P], ident[:, :], rz[:, c:c + 1], None,
                                          ALU.mult).then_inc(norm_done, 1)

            def weights_lo(a):
                for k in range(heads_of(a)):
                    dve.wait_ge(pT_hi_done, heads_before(a) + k + 1)
                    at = pT_at(a, k)
                    dve.tensor_tensor(pT_lo[:, k, :, :].rearrange("p j n -> p (j n)"), ps[:, at:at + 2 * N],
                                      pT_hi[:, k, :, :].rearrange("p j n -> p (j n)").bitcast(F32),
                                      ALU.subtract).then_inc(pT_lo_done, 1)

            def elu(h):
                for q in range(3):
                    pair = z[:, 2 * q * N:(2 * q + 2) * N]
                    dve.wait_ge(elu_exp, 6 * h + 2 * q + 2)
                    dve.tensor_scalar(pair, pair, 1.0, -1.0, ALU.min, ALU.add).then_inc(elu_neg, 1)
                    dve.wait_ge(elu_neg, 3 * h + q + 1)
                    for c in range(2):
                        t = 2 * q + c
                        dve.scalar_tensor_tensor(z[:, t * N:(t + 1) * N],
                                                 ps[:, ELU_AT[q] + c * N:ELU_AT[q] + (c + 1) * N],
                                                 b1_cols[:, bass.ds(KD * h + t, 1)], z[:, t * N:(t + 1) * N],
                                                 ALU.add, ALU.max).then_inc(z_done, 1)
                    if q >= 1:
                        elu_lo(h, q - 1)
                elu_lo(h, 2)

            def elu_lo(h, q):
                dve.wait_ge(z_hi_done, 3 * h + q + 1)
                hi = zT_hi[:, 2 * q:2 * q + 2, :].rearrange("p k n -> p (k n)")
                dve.tensor_tensor(zT_lo[:, 2 * q:2 * q + 2, :].rearrange("p k n -> p (k n)"),
                                  z[:, 2 * q * N:(2 * q + 2) * N], hi.bitcast(F32), ALU.subtract)\
                   .then_inc(z_lo_done, 1)

            for i in range(NT):
                dve.wait_ge(counted, i + 1)
                dve.tensor_copy(counts[:, i, :], ps[:, (6 + i) * BANK:(6 + i) * BANK + N]).then_inc(counts_copied, 1)
            dve.wait_ge(counts_copied, NT)
            for i in range(NT):
                loops = counts[:, i, i * P:(i + 1) * P]
                dve.tensor_tensor(loops, loops, ident[:, :], ALU.add).then_inc(counts_done, 1)
            dve.wait_ge(counts_done, NT)
            dve.tensor_scalar(far[:, :, :], counts[:, :, :], 0.0, FAR, ALU.is_equal, ALU.mult).then_inc(far_done, 1)
            dve.wait_ge(far_done, 1)

            def head(h, first=False):
                if not first:
                    for c in range(POOL_CH, CH):
                        split_lo(dve, 2 * h, c)
                attention(h)
                weights_lo(h)
                for c in range(POOL_CH, CH):
                    split_lo(dve, 2 * h + 1, c)
                elu(h)

            head(0, first=True)
            with dve.Fori(1, H0) as h:
                head(h)

            def layer_stats(n, i, t, width):
                part = width // 2
                for s in range(2):
                    dve.bn_stats(stats[:, i, s, :], t[:, s * part:(s + 1) * part]).then_inc(stats_done, 1)
                dve.wait_ge(stats_done, 2 * (NT * n + i + 1))
                dve.bn_aggr(mv[:, i, :], stats[:, i, :, :]).then_inc(aggr_done, 1)
                dve.wait_ge(aggr_done, NT * n + i + 1)
                dve.tensor_scalar(ve[:, i:i + 1], mv[:, i, 1:2], EPS, None, ALU.add).then_inc(ve_done, 1)

            mine = [q for q in plan if q["who"] == "dve"]
            attention(A_CONV2)
            weights_lo(A_CONV2)
            split_lo1(dve, mine[0])
            y = [z[:, i * D:(i + 1) * D] for i in range(NT)]
            dve.wait_ge(xb_done, NT)
            for i in range(NT):
                dve.wait_ge(nat_done, i + 1)
                dve.tensor_tensor(y[i], ps[:, NAT_AT[i]:NAT_AT[i] + D], x_sb[:, i, :], ALU.add).then_inc(biased, 1)
                dve.wait_ge(biased, i + 1)
                layer_stats(0, i, y[i], D)
            for i in range(NT):
                dve.wait_ge(rstd_done, i + 1)
                dve.tensor_scalar(x_sb[:, i, :], y[i], mv[:, i, 0:1], rstd[:, i:i + 1], ALU.subtract, ALU.mult)\
                   .then_inc(x1_done, 1)
            for i in range(NT):
                dve.wait_ge(x1T_hi_done, i + 1)
                at = ACC + 2 * i * BANK
                dve.tensor_tensor(xT_lo[:, :, i * P:(i + 1) * P], ps[:, at:at + D].rearrange("p (k n) -> p k n", n=P),
                                  xT_hi[:, :, i * P:(i + 1) * P].bitcast(F32), ALU.subtract).then_inc(x1T_lo_done, 1)
            split_lo1(dve, mine[1])
            split_lo1(dve, mine[2])
            attention(A_GAT1)
            split_lo1(dve, mine[3])
            weights_lo(A_GAT1)
            dve.wait_ge(rows_loaded, 16 * 8)
            dve.wait_ge(chunk_used, plan[2 * KD - 1]["n"] + 1)
            dve.wait_ge(h_lo_done, 2 * A_GAT1 + 2)
            for i in range(NT):
                dve.tensor_tensor(hs[:, i * HC:(i + 1) * HC], ps[:, 4 * BANK + i * HC:4 * BANK + (i + 1) * HC],
                                  rows_hc[:, 3, :], ALU.add).then_inc(r_added, 1)
            y1 = [z[:, i * HC:(i + 1) * HC] for i in range(NT)]
            for i in range(NT):
                dve.wait_ge(nat_done, NT + i + 1)
                dve.tensor_tensor(y1[i], ps[:, i * HC:(i + 1) * HC], rows_hc[:, 0, :], ALU.add).then_inc(biased, 1)
                dve.wait_ge(biased, NT + i + 1)
                layer_stats(1, i, y1[i], HC)
            dve.wait_ge(r_added, NT)
            for i in range(NT):
                dve.scalar_tensor_tensor(y1[i], y1[i], mv[:, i, 0:1], rows_hc[:, 1, :], ALU.subtract, ALU.mult)\
                   .then_inc(norm1, 1)
                dve.wait_ge(norm1, i + 1)
                dve.wait_ge(rstd_done, NT + i + 1)
                dve.scalar_tensor_tensor(y1[i], y1[i], rstd[:, i:i + 1], rows_hc[:, 2, :], ALU.mult, ALU.add)\
                   .then_inc(norm2, 1)
                dve.wait_ge(norm2, i + 1)
                dve.scalar_tensor_tensor(y1[i], y1[i], 0.0, hs[:, i * HC:(i + 1) * HC], ALU.max, ALU.add)\
                   .then_inc(h1_done, 1)
            split_lo1(dve, mine[4])
            split_lo1(dve, mine[5])
            for i in range(NT):
                dve.wait_ge(h1T_hi_done, i + 1)
                at = 4 * BANK + i * HC
                dve.tensor_tensor(zT_lo[:, :, i * P:(i + 1) * P], ps[:, at:at + HC].rearrange("p (k n) -> p k n", n=P),
                                  zT_hi[:, :, i * P:(i + 1) * P].bitcast(F32), ALU.subtract).then_inc(h1T_lo_done, 1)
            for q in mine[6:]:
                if q["what"] == "W2" or q["k"] < 4:
                    split_lo1(dve, q)
            attention(A_GAT2)
            weights_lo(A_GAT2)
            for q in mine[6:]:
                if not (q["what"] == "W2" or q["k"] < 4):
                    split_lo1(dve, q)
            dve.wait_ge(chunk_used, plan[-1]["n"] + 1)
            dve.wait_ge(h_lo_done, 2 * A_GAT2 + 2)
            for i in range(NT):
                dve.tensor_tensor(feat(hs, A_GAT2, i), ps[:, 3 * BANK + i * D:3 * BANK + (i + 1) * D],
                                  rows_d[:, 3, :], ALU.add).then_inc(r2_added, 1)
            dve.wait_ge(r2_added, NT)
            for i in range(NT):
                dve.tensor_tensor(feat(hs, A_GAT2, i), feat(hs, A_GAT2, i), x_sb[:, i, :], ALU.add).then_inc(summed, 1)
            for i in range(NT):
                dve.wait_ge(nat_done, 2 * NT + i + 1)
                dve.tensor_tensor(y[i], ps[:, NAT_AT[i]:NAT_AT[i] + D], rows_d[:, 0, :], ALU.add).then_inc(biased, 1)
                dve.wait_ge(biased, 2 * NT + i + 1)
                layer_stats(2, i, y[i], D)
            dve.wait_ge(summed, NT)
            for i in range(NT):
                dve.scalar_tensor_tensor(y[i], y[i], mv[:, i, 0:1], rows_d[:, 1, :], ALU.subtract, ALU.mult)\
                   .then_inc(norm1, 1)
                dve.wait_ge(norm1, NT + i + 1)
                dve.wait_ge(rstd_done, 2 * NT + i + 1)
                dve.scalar_tensor_tensor(y[i], y[i], rstd[:, i:i + 1], rows_d[:, 2, :], ALU.mult, ALU.add)\
                   .then_inc(norm2, 1)
                dve.wait_ge(norm2, NT + i + 1)
                dve.tensor_tensor(y[i], y[i], feat(hs, A_GAT2, i), ALU.add).then_inc(biased, 1)
                dve.wait_ge(biased, 3 * NT + i + 1)
                layer_stats(3, i, y[i], D)
            for i in range(NT):
                dve.wait_ge(rstd_done, 3 * NT + i + 1)
                dve.tensor_scalar(x_sb[:, i, :], y[i], mv[:, i, 0:1], rstd[:, i:i + 1], ALU.subtract, ALU.mult)\
                   .then_inc(out_ready, 1)


INPUTS = ["x", "src", "dst"] \
    + ["L0_gnn_" + n for n in ("W1", "a_src1", "a_dst1", "b1", "W2", "a_src2", "a_dst2", "b2")] \
    + ["L1_gnn_" + n for n in ("W1", "a_src1", "a_dst1", "b1", "g1", "be1", "Wr1", "br1",
                               "W2", "a_src2", "a_dst2", "b2", "g2", "be2", "Wr2", "br2")]


def kernel(**inputs):
    import numpy as np
    import concourse.bacc as bacc
    from concourse.bass_utils import run_bass_kernel_spmd

    nc = bacc.Bacc("TRN2", target_bir_lowering=False, num_devices=1)
    arrays, args = {}, []
    for name in INPUTS:
        a = np.ascontiguousarray(inputs[name])
        arrays[f"in_{name}"] = a
        args.append(nc.dram_tensor(f"in_{name}", a.shape, mybir.dt.from_np(a.dtype), kind="ExternalInput").ap())
    out = nc.dram_tensor("out", (N, D), F32, kind="ExternalOutput").ap()
    build_gnn(nc, *args, out)
    r = run_bass_kernel_spmd(nc, [arrays], core_ids=[0])
    return r.results[0]["out"]
```

```python
from contextlib import ExitStack

import concourse.bass as bass
from concourse import mybir

ALU = mybir.AluOpType
ACT = mybir.ActivationFunctionType
F32 = mybir.dt.float32
F32R = mybir.dt.float32r
BF16 = mybir.dt.bfloat16
I32 = mybir.dt.int32

P = 128
N = 256
NT = N // P
D = 768
KD = D // P
H0 = 8
H1, C1 = 4, 256
HC = H1 * C1
KH = HC // P
E = 4096
ET = E // P
BANK = 512
SLOPE = 0.2
EPS = 1e-5
FAR = -1.0e30

CH = KD
RG = 3
POOL_CH = 4
DVE_CH = CH - POOL_CH
PHASES = 2 * H0

A_CONV2, A_GAT1A, A_GAT1B, A_GAT2 = H0, H0 + 1, H0 + 2, H0 + 3
HH = H1 // 2
HW = HH * C1


def block1_plan():
    plan = []
    pool, dve = POOL_CH * PHASES, DVE_CH * PHASES
    loads = [PHASES] * RG
    free_at = [("pool", pool - 2), ("pool", pool), ("dve", dve)]
    used0 = CH * PHASES

    def group(what, part, k, width, who, slots, used):
        nonlocal pool, dve
        g = group.n % RG
        group.n += 1
        loads[g] += 1
        free = free_at[g]
        for m, (slot, need) in enumerate(zip(slots, used)):
            if who == "dve":
                dve += 1
            else:
                pool += 1
            plan.append(dict(what=what, part=part, k=k + m, width=width, raw_group=g, raw_at=m * width,
                             first=m == 0, chunks=len(slots), free=free, full=16 * loads[g],
                             ring_at=slot * width, used=need, who=who,
                             lo=dve if who == "dve" else pool, n=used0 + len(plan)))
        free_at[g] = (who, dve if who == "dve" else pool)

    group.n = 0
    slots_w = CH * D // HW
    wide = 4 * KD
    for i in range(0, wide, 3):
        slots, needs = [], []
        for j in range(i, i + 3):
            slots.append(j % slots_w)
            if j < slots_w:
                needs.append(used0 - CH + (HW * (j + 1) - 1) // D + 1)
            else:
                needs.append(used0 + j - slots_w + 1)
        half, k = divmod(i, KD)
        group("W1" if half < 2 else "Wr1", half % 2, k, HW, "dve" if i in (6, 9) else "pool", slots, needs)
    for i in range(0, 2 * KH, 2):
        slots, needs = [], []
        for j in (i, i + 1):
            slot = (j + 4) % CH
            slots.append(slot)
            if j < CH:
                lo, hi = D * slot // HW, (D * (slot + 1) - 1) // HW
                needs.append(used0 + max(max(m for m in range(wide) if m % slots_w == v)
                                         for v in range(lo, hi + 1)) + 1)
            else:
                needs.append(used0 + wide + j - CH + 1)
        group("W2" if i < KH else "Wr2", 0, i % KH, D, "dve" if i in (6, 10) else "pool", slots, needs)
    return plan


def build_gnn(nc, x, src, dst, b0_W1, b0_as1, b0_ad1, b0_b1, b0_W2, b0_as2, b0_ad2, b0_b2,
              b1_W1, b1_as1, b1_ad1, b1_b1, b1_g1, b1_be1, b1_Wr1, b1_br1,
              b1_W2, b1_as2, b1_ad2, b1_b2, b1_g2, b1_be2, b1_Wr2, b1_br2, out):
    plan = block1_plan()
    wide_chunks = 2 * KD
    ctx = ExitStack()
    with ctx:
        def sb(name, shape, dt=F32):
            return ctx.enter_context(nc.sbuf_tensor(name, shape, dt))

        def sem(name):
            return ctx.enter_context(nc.semaphore(name))

        x_sb = sb("x_sb", [P, NT, D])
        xT_hi = sb("xT_hi", [P, KD, N], F32R)
        xT_lo = sb("xT_lo", [P, KD, N], F32R)
        counts = sb("counts", [P, NT, N])
        far = sb("far", [P, NT, N])
        ident = sb("ident", [P, P])
        zeros = sb("zeros", [P, P], BF16)
        iota = sb("iota", [P, N], BF16)
        edges = sb("edges", [P, 2, ET], I32)
        edges_f = sb("edges_f", [P, 2, ET])
        raw = sb("raw", [P, RG, 2 * D])
        ring_hi = sb("ring_hi", [P, CH * D], F32R)
        ring_lo = sb("ring_lo", [P, CH * D], F32R)
        att = sb("att", [P, 2 * HC])
        hs = sb("hs", [P, NT * HC])
        h_hi = sb("h_hi", [P, NT * HC], F32R)
        h_lo = sb("h_lo", [P, NT * HC], F32R)
        pT_hi = sb("pT_hi", [P, H1, NT, N], F32R)
        pT_lo = sb("pT_lo", [P, H1, NT, N], F32R)
        zT_hi = sb("zT_hi", [P, KH, N], F32R)
        zT_lo = sb("zT_lo", [P, KH, N], F32R)
        z = sb("z", [P, KH * N])
        am = sb("am", [P, H1, NT, N])
        e1 = sb("e1", [P, H1, NT, N])
        e2 = sb("e2", [P, H1, NT, N])
        b1_cols = sb("b1_cols", [P, H0 * KD])
        b1_rows = sb("b1_rows", [H0 * KD, P])
        rows_hc = sb("rows_hc", [P, 4, HC])
        rows_d = sb("rows_d", [P, 4, D])
        S = 2 * H1
        a_s = sb("a_s", [P, S])
        a_d = sb("a_d", [P, S])
        a_d2 = sb("a_d2", [P, S])
        mx = sb("mx", [P, S])
        zc = sb("zc", [P, S])
        mm = sb("mm", [P, S])
        bias1 = sb("bias1", [P, S])
        bias2 = sb("bias2", [P, S])
        zsum = sb("zsum", [P, S])
        rz = sb("rz", [P, S])
        stats = sb("stats", [P, NT, 2, 6])
        mv = sb("mv", [P, NT, 2])
        ve = sb("ve", [P, NT])
        rstd = sb("rstd", [P, NT])
        half = sb("half", [P, 1])

        hot_homes = [t.bitcast(BF16) for t in (am[:].rearrange("p a b c -> p (a b c)"),
                                               z[:], rows_hc[:, 0:2, :].rearrange("p a c -> p (a c)"),
                                               rows_hc[:, 2:4, :].rearrange("p a c -> p (a c)"))]
        per_home = ET // len(hot_homes)

        def hot(t, which):
            at = ((t % per_home) * 2 + which) * N
            return hot_homes[t // per_home][:, at:at + N]

        iota_i = hs[:, 0:N].bitcast(I32)

        ps = ctx.enter_context(nc.psum_tensor("ps", [P, 8 * BANK], F32))
        PROJ, ACC = 0, 3 * BANK
        S_AT, T_AT = 6 * BANK, 7 * BANK
        NAT_AT = [0, 6 * BANK]
        X1T_AT = [3 * BANK, 4 * BANK, 5 * BANK]
        H1T_AT = [4 * BANK, 6 * BANK, 5 * BANK, 7 * BANK]
        ELU_AT = [2 * BANK, 6 * BANK, 7 * BANK]

        raw_full = [sem(f"raw_full{g}") for g in range(RG)]
        hi_done = sem("hi_done")
        lo_by = {"pool": sem("lo_pool"), "dve": sem("lo_dve")}
        chunk_used = sem("chunk_used")
        x_loaded = sem("x_loaded")
        b2_loaded = sem("b2_loaded")
        edges_loaded = sem("edges_loaded")
        b1_loaded = sem("b1_loaded")
        rows_loaded = sem("rows_loaded")
        att_loaded = sem("att_loaded")
        consts = sem("consts")
        table_loaded = sem("table_loaded")
        iota_ready = sem("iota_ready")
        xT_ps = sem("xT_ps")
        xT_hi_done = sem("xT_hi_done")
        xT_lo_done = sem("xT_lo_done")
        edges_cast = sem("edges_cast")
        hot_done = sem("hot_done")
        counted = sem("counted")
        counts_copied = sem("counts_copied")
        counts_done = sem("counts_done")
        far_done = sem("far_done")
        b1_ps = sem("b1_ps")
        b1_ready = sem("b1_ready")
        xb_done = sem("xb_done")
        hs_done = sem("hs_done")
        h_hi_done = sem("h_hi_done")
        h_lo_done = sem("h_lo_done")
        a_src_done = sem("a_src_done")
        a_dst_done = sem("a_dst_done")
        scores_bc = sem("scores_bc")
        slope_done = sem("slope_done")
        masked = sem("masked")
        top_done = sem("top_done")
        m_done = sem("m_done")
        bias_done = sem("bias_done")
        exps_done = sem("exps_done")
        emax_done = sem("emax_done")
        p_done = sem("p_done")
        rz_done = sem("rz_done")
        norm_done = sem("norm_done")
        pT_ps = sem("pT_ps")
        pT_hi_done = sem("pT_hi_done")
        pT_lo_done = sem("pT_lo_done")
        agg_done = sem("agg_done")
        elu_exp = sem("elu_exp")
        elu_neg = sem("elu_neg")
        z_done = sem("z_done")
        z_hi_done = sem("z_hi_done")
        z_lo_done = sem("z_lo_done")
        nat_done = sem("nat_done")
        biased = sem("biased")
        stats_done = sem("stats_done")
        aggr_done = sem("aggr_done")
        ve_done = sem("ve_done")
        rstd_done = sem("rstd_done")
        norm1 = sem("norm1")
        norm2 = sem("norm2")
        x1_done = sem("x1_done")
        x1T_ps = sem("x1T_ps")
        x1T_hi_done = sem("x1T_hi_done")
        x1T_lo_done = sem("x1T_lo_done")
        r_added = sem("r_added")
        h1_done = sem("h1_done")
        h1T_ps = sem("h1T_ps")
        h1T_hi_done = sem("h1T_hi_done")
        h1T_lo_done = sem("h1T_lo_done")
        r2_added = sem("r2_added")
        shifted = sem("shifted")
        out_ready = sem("out_ready")
        stored = sem("stored")

        block = ctx.enter_context(nc.Block())

        def slot_hi(c):
            return ring_hi[:, c * D:(c + 1) * D]

        def slot_lo(c):
            return ring_lo[:, c * D:(c + 1) * D]

        def raw_chunk(c):
            return raw[:, c // 2, (c % 2) * D:(c % 2 + 1) * D]

        def split_hi(eng, p, c, reused=True):
            if c % 2 == 0:
                eng.wait_ge(raw_full[c // 2], 16 * p + 16)
            if reused:
                eng.wait_ge(chunk_used, CH * p + c - CH + 1)
            eng.activation(slot_hi(c), raw_chunk(c), ACT.Copy).then_inc(hi_done, 1)

        def split_lo(eng, p, c):
            eng.wait_ge(hi_done, CH * p + c + 1)
            eng.tensor_tensor(slot_lo(c), raw_chunk(c), slot_hi(c).bitcast(F32), ALU.subtract)\
               .then_inc(lo_by["pool" if c < POOL_CH else "dve"], 1)

        def split_hi1(eng, q):
            if q["first"]:
                eng.wait_ge(raw_full[q["raw_group"]], q["full"])
            eng.wait_ge(chunk_used, q["used"])
            w = q["width"]
            eng.activation(ring_hi[:, q["ring_at"]:q["ring_at"] + w],
                           raw[:, q["raw_group"], q["raw_at"]:q["raw_at"] + w], ACT.Copy)\
               .then_inc(hi_done, 1)

        def split_lo1(eng, q):
            eng.wait_ge(hi_done, q["n"] + 1)
            w = q["width"]
            eng.tensor_tensor(ring_lo[:, q["ring_at"]:q["ring_at"] + w],
                              raw[:, q["raw_group"], q["raw_at"]:q["raw_at"] + w],
                              ring_hi[:, q["ring_at"]:q["ring_at"] + w].bitcast(F32), ALU.subtract)\
               .then_inc(lo_by[q["who"]], 1)

        def is_gat1(a):
            return isinstance(a, int) and a in (A_GAT1A, A_GAT1B)

        def heads_of(a):
            return HH if is_gat1(a) else 1

        def first_head(a):
            return HH * (a - A_GAT1A) if is_gat1(a) else 0

        def feat(t, a, i):
            if is_gat1(a):
                at = i * HC + (a - A_GAT1A) * HW
                return t[:, at:at + HW]
            return t[:, i * D:(i + 1) * D]

        def source_at(a, i):
            if is_gat1(a):
                at = i * HC + (a - A_GAT1A) * HW
                return ps[:, at:at + HW]
            at = (ACC if isinstance(a, int) and a == A_CONV2 else PROJ) + i * D
            return ps[:, at:at + D]

        def pT_at(a, k):
            return (2 - 2 * k + a - A_GAT1A) * BANK if is_gat1(a) else T_AT

        def s_at(a, k):
            return (a - A_GAT1A) * BANK + k * N if is_gat1(a) else S_AT

        def elu_at(h, q):
            if isinstance(h, int) and h == 0:
                return ELU_AT[(q + 1) % 3]
            return ELU_AT[q]

        def heads_before(a):
            return a if not isinstance(a, int) or a <= A_GAT1A else a + min(a - A_GAT1A, 2) * (HH - 1)

        def before(a):
            return 2 * heads_before(a)

        def scaled_late(a):
            return isinstance(a, int) and a >= A_CONV2

        PASSES = 3

        def three(hi_a, lo_a, hi_b, lo_b):
            return ((hi_a, hi_b), (hi_a, lo_b), (lo_a, hi_b))

        @block.sync
        def _(sp):
            w1 = b0_W1.rearrange("(k p) (h c) -> p k h c", p=P, c=D)
            w2 = b0_W2.rearrange("(h k p) c -> p h k c", p=P, k=KD)

            def load(p, g, view):
                dst_ap = raw[:, g, :].rearrange("p (k c) -> p k c", k=2)
                sp.dma_start(dst_ap, view).then_inc(raw_full[g], 16)

            def load_phase(p, view, reused=True):
                for g in range(RG):
                    if reused:
                        if g < RG - 1:
                            sp.wait_ge(lo_by["pool"], POOL_CH * p - POOL_CH + 2 * (g + 1))
                        else:
                            sp.wait_ge(lo_by["dve"], DVE_CH * p)
                    load(p, g, view(g))

            def w1_of(h):
                return lambda g: w1[:, 2 * g:2 * g + 2, bass.ds(h, 1), :].rearrange("p k h c -> p k (h c)")

            def w2_of(h):
                return lambda g: w2[:, bass.ds(h, 1), 2 * g:2 * g + 2, :].rearrange("p h k c -> p (h k) c")

            sp.dma_start(x_sb[:, :, :], x.rearrange("(t p) c -> p t c", p=P)).then_inc(x_loaded, 16)
            load_phase(0, w1_of(0), reused=False)
            load_phase(1, w1_of(1))
            load_phase(2, w2_of(0))
            with sp.Fori(2, H0) as h:
                load_phase(2 * h - 1, w1_of(h))
                load_phase(2 * h, w2_of(h - 1))
            load_phase(PHASES - 1, w2_of(H0 - 1))
            views = {"W1": b1_W1, "Wr1": b1_Wr1, "W2": b1_W2, "Wr2": b1_Wr2}
            for q in plan:
                if not q["first"]:
                    continue
                who, count = q["free"]
                sp.wait_ge(lo_by[who], count)
                at = q["part"] * q["width"]
                view = views[q["what"]].rearrange("(k p) c -> p k c", p=P)[:, q["k"]:q["k"] + q["chunks"],
                                                                          at:at + q["width"]]
                width = q["chunks"] * q["width"]
                sp.dma_start(raw[:, q["raw_group"], 0:width].rearrange("p (k c) -> p k c", k=q["chunks"]),
                             view).then_inc(raw_full[q["raw_group"]], 16)
            for i in range(NT):
                sp.wait_ge(out_ready, i + 1)
                sp.dma_start(out[i * P:(i + 1) * P, :], x_sb[:, i, :]).then_inc(stored, 16)
            sp.wait_ge(stored, 16 * NT)

        @block.gpsimd
        def _(pool):
            pool.memset(ident[:, :], 0.0).then_inc(consts, 1)
            pool.wait_ge(consts, 1)
            pool.affine_select(out=ident[:, :], in_=ident[:, :], compare_op=ALU.not_equal, fill=1.0,
                               base=0, pattern=[[-1, P]], channel_multiplier=1).then_inc(consts, 1)
            pool.iota(iota_i, pattern=[[1, N]], base=0, channel_multiplier=0).then_inc(iota_ready, 1)
            pool.memset(zeros[:, :], 0.0).then_inc(consts, 1)
            pool.memset(half[:, :], -0.5).then_inc(consts, 1)
            for c in range(POOL_CH):
                split_lo(pool, 0, c)

            def features_lo(a):
                for i in range(NT):
                    pool.wait_ge(h_hi_done, 2 * a + i + 1)
                    pool.tensor_tensor(feat(h_lo, a, i), feat(hs, a, i), feat(h_hi, a, i).bitcast(F32),
                                       ALU.subtract).then_inc(h_lo_done, 1)

            def phase_lo(p):
                for c in range(POOL_CH):
                    split_lo(pool, p, c)

            def head(h):
                phase_lo(2 * h)
                features_lo(h)
                phase_lo(2 * h + 1)

            phase_lo(1)
            features_lo(0)
            pool.wait_ge(b2_loaded, 16)
            pool.wait_ge(xT_ps, 3)
            for i in range(NT):
                pool.tensor_tensor(x_sb[:, i, :], x_sb[:, i, :], rows_d[:, 3, :], ALU.add).then_inc(xb_done, 1)
            with pool.Fori(1, H0) as h:
                head(h)

            def inverse_root(n, i):
                pool.wait_ge(ve_done, NT * n + i + 1)
                pool.tensor_tensor(rstd[:, i:i + 1], ve[:, i:i + 1], half[:, :], ALU.pow).then_inc(rstd_done, 1)

            mine = [q for q in plan if q["who"] == "pool"]
            wide = [q for q in mine if q["width"] == HW]
            narrow = [q for q in mine if q["width"] == D]
            for q in wide[:6]:
                split_lo1(pool, q)
            features_lo(A_CONV2)
            for i in range(NT):
                inverse_root(0, i)
            for q in wide[6:9]:
                split_lo1(pool, q)
            features_lo(A_GAT1A)
            for q in wide[9:12]:
                split_lo1(pool, q)
            features_lo(A_GAT1B)
            for q in wide[12:]:
                split_lo1(pool, q)
            for q in narrow[:3]:
                split_lo1(pool, q)
            for i in range(NT):
                inverse_root(1, i)
            for q in narrow[3:10]:
                split_lo1(pool, q)
            features_lo(A_GAT2)
            for q in narrow[10:]:
                split_lo1(pool, q)
            for n in (2, 3):
                for i in range(NT):
                    inverse_root(n, i)

        @block.scalar
        def _(act):
            def load_att(n, a_src, a_dst, width, reused=True):
                if reused:
                    act.wait_ge(a_dst_done, 2 * n)
                for half_at, v in ((0, a_src), (1, a_dst)):
                    act.dma_start(att[:, half_at * width:(half_at + 1) * width], v.partition_broadcast(P))\
                       .then_inc(att_loaded, 16)

            def att_row(t, h):
                return t[bass.ds(h, 1), :]

            act.dma_start(edges[:, 0, :], src.rearrange("(p t) -> p t", p=P)).then_inc(edges_loaded, 16)
            act.dma_start(edges[:, 1, :], dst.rearrange("(p t) -> p t", p=P)).then_inc(edges_loaded, 16)
            act.dma_start(b1_rows[:, :], b0_b1.rearrange("(t p) -> t p", p=P)).then_inc(b1_loaded, 16)
            load_att(0, b0_as1[0:1, :], b0_ad1[0:1, :], D, reused=False)

            act.wait_ge(consts, 4)
            act.activation(rstd[:, 0:1], half[:, :], ACT.Exp).then_inc(table_loaded, 1)

            for b in range(3):
                act.wait_ge(xT_ps, b + 1)
                act.activation(xT_hi[:, 2 * b:2 * b + 2, :].rearrange("p k n -> p (k n)"),
                               ps[:, (5 + b) * BANK:(6 + b) * BANK], ACT.Copy).then_inc(xT_hi_done, 1)
            for c in range(CH):
                split_hi(act, 0, c, reused=False)
            act.dma_start(rows_d[:, 3, :], b0_b2.partition_broadcast(P)).then_inc(b2_loaded, 16)

            def features_copy(a, chunks):
                act.wait_ge(chunk_used, chunks)
                for i in range(NT):
                    act.activation(feat(hs, a, i), source_at(a, i), ACT.Copy).then_inc(hs_done, 1)

            def features_hi(a):
                for i in range(NT):
                    act.wait_ge(hs_done, 2 * a + i + 1)
                    act.activation(feat(h_hi, a, i), feat(hs, a, i), ACT.Copy).then_inc(h_hi_done, 1)

            def exps(a):
                act.wait_ge(bias_done, 2 * a + 2)
                for k in range(first_head(a), first_head(a) + heads_of(a)):
                    for i in range(NT):
                        c = 2 * k + i
                        act.activation(e1[:, k, i, :], am[:, k, i, :], ACT.Exp, bias=bias1[:, c:c + 1])\
                           .then_inc(exps_done, 1)
                        act.activation(e2[:, k, i, :], am[:, k, i, :], ACT.Exp, bias=bias2[:, c:c + 1],
                                       scale=SLOPE).then_inc(exps_done, 1)

            def weights_hi(a):
                for k in range(heads_of(a)):
                    act.wait_ge(pT_ps, heads_before(a) + k + 1)
                    at = pT_at(a, k)
                    act.activation(pT_hi[:, first_head(a) + k, :, :].rearrange("p j n -> p (j n)"),
                                   ps[:, at:at + 2 * N], ACT.Copy).then_inc(pT_hi_done, 1)

            def elu(h, first=False):
                for q in range(3):
                    act.wait_ge(agg_done, 3 * h + q + 1)
                    if not first:
                        act.wait_ge(z_lo_done, 3 * h + q - 2)
                    for c in range(2):
                        t = 2 * q + c
                        at = elu_at(h, q) + c * N
                        act.activation(z[:, t * N:(t + 1) * N], ps[:, at:at + N], ACT.Exp,
                                       bias=b1_cols[:, bass.ds(KD * h + t, 1)]).then_inc(elu_exp, 1)
                    if q >= 1:
                        elu_hi(h, q - 1)
                elu_hi(h, 2)

            def elu_hi(h, q):
                act.wait_ge(z_done, 6 * h + 2 * q + 2)
                act.activation(zT_hi[:, 2 * q:2 * q + 2, :].rearrange("p k n -> p (k n)"),
                               z[:, 2 * q * N:(2 * q + 2) * N], ACT.Copy).then_inc(z_hi_done, 1)

            def att_for(h, last=False):
                if last:
                    load_att(h, b0_as2[0:1, :], b0_ad2[0:1, :], D)
                else:
                    load_att(h, att_row(b0_as1, h), att_row(b0_ad1, h), D)

            def softmax_and_elu(h, last=False):
                for c in (0, 1):
                    split_hi(act, 2 * h + 1, c)
                att_for(h + 1, last)
                exps(h)
                for c in (2, 3):
                    split_hi(act, 2 * h + 1, c)
                weights_hi(h)
                for c in (4, 5):
                    split_hi(act, 2 * h + 1, c)
                elu(h)

            def head(h, last=False):
                for c in range(CH - 1):
                    split_hi(act, 2 * h, c)
                features_copy(h, 2 * CH * h)
                split_hi(act, 2 * h, CH - 1)
                features_hi(h)
                softmax_and_elu(h, last)

            for c in range(4):
                split_hi(act, 1, c)
            features_copy(0, CH)
            for c in (4, 5):
                split_hi(act, 1, c)
            features_hi(0)
            att_for(1)
            exps(0)
            act.wait_ge(counted, NT)
            for n, v in enumerate((b1_b1, b1_g1, b1_be1, b1_br1)):
                act.dma_start(rows_hc[:, n, :], v.partition_broadcast(P)).then_inc(rows_loaded, 16)
            for n, v in enumerate((b1_b2, b1_g2, b1_be2)):
                act.dma_start(rows_d[:, n, :], v.partition_broadcast(P)).then_inc(rows_loaded, 16)
            for c in (0, 1, 2):
                split_hi(act, 2, c)
            weights_hi(0)
            for c in (3, 4, 5):
                split_hi(act, 2, c)
            act.wait_ge(h_lo_done, 2)
            features_copy(1, 2 * CH)
            act.wait_ge(b1_ready, 1)
            elu(0, first=True)
            features_hi(1)
            softmax_and_elu(1)
            with act.Fori(2, H0 - 1) as h:
                head(h)
            head(H0 - 1, last=True)

            act.wait_ge(xb_done, NT)
            act.dma_start(rows_d[:, 3, :], b1_br2.partition_broadcast(P)).then_inc(rows_loaded, 16)

            def chunks_hi(first, end):
                for q in plan[first:end]:
                    split_hi1(act, q)

            chunks_hi(0, 6)
            features_copy(A_CONV2, CH * PHASES)
            features_hi(A_CONV2)
            load_att(A_GAT1A, b1_as1.rearrange("h c -> (h c)"), b1_ad1.rearrange("h c -> (h c)"), HC)
            exps(A_CONV2)
            weights_hi(A_CONV2)
            chunks_hi(6, 9)
            for b in range(KD // 2):
                act.wait_ge(x1T_ps, b + 1)
                act.activation(xT_hi[:, 2 * b:2 * b + 2, :].rearrange("p k n -> p (k n)"),
                               ps[:, X1T_AT[b]:X1T_AT[b] + 2 * N], ACT.Copy).then_inc(x1T_hi_done, 1)
            chunks_hi(9, 14)
            features_copy(A_GAT1A, plan[KD - 1]["n"] + 1)
            chunks_hi(14, 15)
            features_hi(A_GAT1A)
            chunks_hi(15, 19)
            exps(A_GAT1A)
            features_copy(A_GAT1B, plan[2 * KD - 1]["n"] + 1)
            chunks_hi(19, 21)
            weights_hi(A_GAT1A)
            chunks_hi(21, 22)
            features_hi(A_GAT1B)
            chunks_hi(22, 25)
            act.wait_ge(a_dst_done, before(A_GAT2))
            for half_at, v in ((0, b1_as2), (1, b1_ad2)):
                act.dma_start(att[:, half_at * D:(half_at + 1) * D], v[0:1, :].partition_broadcast(P))\
                   .then_inc(att_loaded, 16)
            exps(A_GAT1B)
            chunks_hi(25, 26)
            weights_hi(A_GAT1B)
            chunks_hi(26, 30)

            def h1_hi(b):
                act.wait_ge(h1T_ps, b + 1)
                act.activation(zT_hi[:, 2 * b:2 * b + 2, :].rearrange("p k n -> p (k n)"),
                               ps[:, H1T_AT[b]:H1T_AT[b] + 2 * N], ACT.Copy).then_inc(h1T_hi_done, 1)

            h1_hi(0)
            h1_hi(1)
            chunks_hi(30, 31)
            h1_hi(2)
            h1_hi(3)
            chunks_hi(31, 37)
            features_copy(A_GAT2, plan[4 * KD + KH - 1]["n"] + 1)
            chunks_hi(37, 38)
            features_hi(A_GAT2)
            chunks_hi(38, 40)
            exps(A_GAT2)
            weights_hi(A_GAT2)

        @block.tensor
        def _(pe):
            def pieces(i):
                return ((0, BANK, 0), (BANK, D, BANK)) if i == 0 else ((0, N, D), (N, D, 2 * BANK))

            def product(at, i, lhs_hi, lhs_lo, w_hi, w_lo, start, stop, bank2_wait=None):
                last = None
                for n, (a, b) in enumerate(three(lhs_hi, lhs_lo, w_hi, w_lo)):
                    for lo, hi, to in pieces(i):
                        if to == 2 * BANK and n == 0 and bank2_wait is not None:
                            pe.wait_ge(*bank2_wait)
                        last = pe.matmul(ps[:, at + to:at + to + hi - lo], a, b[:, lo:hi],
                                         start=start and n == 0 and to != D,
                                         stop=stop and n == PASSES - 1, skip_group_check=True)
                return last

            def chunk(p, c):
                if c < POOL_CH:
                    pe.wait_ge(lo_by["pool"], POOL_CH * p + c + 1)
                else:
                    pe.wait_ge(lo_by["dve"], DVE_CH * p + c - POOL_CH + 1)

            def node_tile(t, k, i):
                return t[:, k, i * P:(i + 1) * P]

            def project_chunk(p, h, c, loop=False):
                chunk(p, c)
                for i in range(NT):
                    wait = (z_done, 6 * h - 4) if c == 0 and i == 1 and loop else None
                    last = product(PROJ, i, node_tile(xT_hi, c, i), node_tile(xT_lo, c, i),
                                   slot_hi(c), slot_lo(c), c == 0, c == CH - 1, wait)
                last.then_inc(chunk_used, 1)

            def accumulate(p, h, c, last_head=False):
                if c % 2 == 0:
                    pe.wait_ge(z_lo_done, 3 * h + c // 2 + 1)
                chunk(p, c)
                for i in range(NT):
                    last = product(ACC, i, node_tile(zT_hi, c, i), node_tile(zT_lo, c, i),
                                   slot_hi(c), slot_lo(c), False, last_head and c == CH - 1)
                last.then_inc(chunk_used, 1)

            def scores(a):
                pe.wait_ge(a_src_done, before(a) + 2 * heads_of(a))
                for k in range(heads_of(a)):
                    for j in range(NT):
                        c, at = 2 * (first_head(a) + k) + j, s_at(a, k) + j * P
                        last = pe.transpose(ps[:, at:at + P], a_s[:, c:c + 1].to_broadcast([P, P]), ident[:, :])
                last.then_inc(scores_bc, 1)

            def weights(a):
                for k in range(heads_of(a)):
                    if scaled_late(a):
                        pe.wait_ge(p_done, before(a) + 2 * (k + 1))
                    else:
                        pe.wait_ge(norm_done, before(a) + 2 * (k + 1))
                    t = e2 if scaled_late(a) else am
                    for j in range(NT):
                        for i in range(NT):
                            at = pT_at(a, k) + j * N + i * P
                            last = pe.transpose(ps[:, at:at + P], t[:, first_head(a) + k, i, j * P:(j + 1) * P],
                                                ident[:, :])
                    last.then_inc(pT_ps, 1)

            def aggregate_T(h):
                pe.wait_ge(h_lo_done, 2 * h + 2)
                pe.wait_ge(pT_lo_done, h + 1)
                for q in range(3):
                    if elu_at(h, q) == ELU_AT[0] and isinstance(h, int) and h == 0:
                        pe.wait_ge(hs_done, 4)
                    for c in range(2):
                        ch = (2 * q + c) * P
                        at = elu_at(h, q) + c * N
                        for j in range(NT):
                            f = [feat(t, 0, j)[:, ch:ch + P] for t in (h_hi, h_lo)]
                            for n, (a, b) in enumerate(three(*f, pT_hi[:, 0, j, :], pT_lo[:, 0, j, :])):
                                last = pe.matmul(ps[:, at:at + N], a, b,
                                                 start=c == 0 and j == 0 and n == 0,
                                                 stop=j == NT - 1 and n == PASSES - 1, skip_group_check=True)
                    last.then_inc(agg_done, 1)

            def aggregate(a):
                pe.wait_ge(h_lo_done, 2 * a + 2)
                pe.wait_ge(pT_lo_done, heads_before(a) + 1)
                for i in range(NT):
                    for j in range(NT):
                        w = [t[:, 0, j, i * P:(i + 1) * P] for t in (pT_hi, pT_lo)]
                        for n, (l, r) in enumerate(three(*w, feat(h_hi, a, j), feat(h_lo, a, j))):
                            for lo, hi in ((0, BANK), (BANK, D)):
                                last = pe.matmul(ps[:, NAT_AT[i] + lo:NAT_AT[i] + hi], l, r[:, lo:hi],
                                                 start=j == 0 and n == 0, stop=j == NT - 1 and n == PASSES - 1)
                    last.then_inc(nat_done, 1)

            pe.wait_ge(consts, 4)
            pe.wait_ge(x_loaded, 16)
            for b in range(3):
                for k in (2 * b, 2 * b + 1):
                    for i in range(NT):
                        at = 5 * BANK + k * N + i * P
                        last = pe.transpose(ps[:, at:at + P], x_sb[:, i, k * P:(k + 1) * P], ident[:, :])
                last.then_inc(xT_ps, 1)
            pe.wait_ge(b1_loaded, 16)
            pe.transpose(ps[:, 3 * BANK:3 * BANK + H0 * KD], b1_rows[:, :], ident[0:H0 * KD, 0:H0 * KD])\
              .then_inc(b1_ps, 1)
            for c in range(CH):
                if c % 2 == 0:
                    pe.wait_ge(xT_lo_done, c // 2 + 1)
                project_chunk(0, 0, c)
            pe.wait_ge(xT_lo_done, 3)
            for i in range(NT):
                for t in range(ET):
                    if i == 0 and t % per_home == 0:
                        pe.wait_ge(hot_done, 2 * (t + per_home))
                    last = pe.matmul(ps[:, (6 + i) * BANK:(6 + i) * BANK + N], hot(t, 1)[:, i * P:(i + 1) * P],
                                     hot(t, 0), start=t == 0, stop=t == ET - 1)
                last.then_inc(counted, 1)
            pe.wait_ge(b1_ready, 1)
            for b in range(3):
                for part in range(2):
                    at = ACC + b * BANK + part * N
                    pe.matmul(ps[:, at:at + N], zeros[:, :], iota[:, :], start=part == 0, stop=False,
                              skip_group_check=True)
            for c in range(CH):
                if c == 1:
                    pe.wait_ge(counts_copied, 2)
                    scores(0)
                if c == 4:
                    weights(0)
                if c == 0:
                    pe.wait_ge(hs_done, NT)
                project_chunk(1, 1, c)
            aggregate_T(0)

            def rest_of_head(h):
                for c in range(CH):
                    if c == 2:
                        pe.wait_ge(z_done, 6 * h)
                        scores(h)
                    if c == 5:
                        weights(h)
                    accumulate(2 * h, h - 1, c)
                aggregate_T(h)

            rest_of_head(1)
            with pe.Fori(2, H0) as h:
                for c in range(CH):
                    project_chunk(2 * h - 1, h, c, loop=True)
                rest_of_head(h)
            for c in range(CH):
                accumulate(PHASES - 1, H0 - 1, c, last_head=True)

            pe.wait_ge(z_done, 6 * H0)
            scores(A_CONV2)
            weights(A_CONV2)
            aggregate(A_CONV2)
            for i in range(NT):
                pe.wait_ge(x1_done, i + 1)
                for k in range(KD):
                    at = X1T_AT[k // 2] + k % 2 * N + i * P
                    last = pe.transpose(ps[:, at:at + P], x_sb[:, i, k * P:(k + 1) * P], ident[:, :])
                    if i == NT - 1 and k % 2 == 1:
                        last.then_inc(x1T_ps, 1)

            def wide_product(q, at):
                pe.wait_ge(lo_by[q["who"]], q["lo"])
                k, w = q["k"], q["ring_at"]
                for i in range(NT):
                    to = at + i * HC + q["part"] * HW
                    for n, (a, b) in enumerate(three(node_tile(xT_hi, k, i), node_tile(xT_lo, k, i),
                                                     ring_hi[:, w:w + HW], ring_lo[:, w:w + HW])):
                        last = pe.matmul(ps[:, to:to + HW], a, b, start=k == 0 and n == 0,
                                         stop=k == KD - 1 and n == PASSES - 1)
                last.then_inc(chunk_used, 1)

            def narrow_product(q, at):
                pe.wait_ge(lo_by[q["who"]], q["lo"])
                k, w = q["k"], q["ring_at"]
                for i in range(NT):
                    last = product(at, i, node_tile(zT_hi, k, i), node_tile(zT_lo, k, i),
                                   ring_hi[:, w:w + D], ring_lo[:, w:w + D], k == 0, k == KH - 1)
                last.then_inc(chunk_used, 1)

            w1a, w1b, wr1a, wr1b = (plan[n * KD:(n + 1) * KD] for n in range(4))
            for q in w1a:
                if q["k"] % 2 == 0:
                    pe.wait_ge(x1T_lo_done, q["k"] // 2 + 1)
                wide_product(q, 0)
            for q in w1b:
                if q["k"] == 2:
                    scores(A_GAT1A)
                wide_product(q, 0)

            def aggregate_half(a):
                pe.wait_ge(h_lo_done, 2 * a + 2)
                pe.wait_ge(pT_lo_done, heads_before(a) + HH)
                for i in range(NT):
                    for k in range(HH):
                        for j in range(NT):
                            f = [feat(t, a, j)[:, k * C1:(k + 1) * C1] for t in (h_hi, h_lo)]
                            w = [t[:, first_head(a) + k, j, i * P:(i + 1) * P] for t in (pT_hi, pT_lo)]
                            for n, (l, r) in enumerate(three(*w, *f)):
                                to = i * HC + (a - A_GAT1A) * HW + k * C1
                                last = pe.matmul(ps[:, to:to + C1], l, r, start=k == 0 and j == 0 and n == 0,
                                                 stop=j == NT - 1 and n == PASSES - 1, skip_group_check=True)
                    last.then_inc(nat_done, 1)

            for q in wr1a:
                if q["k"] == 2:
                    weights(A_GAT1A)
                if q["k"] == 4:
                    scores(A_GAT1B)
                wide_product(q, 4 * BANK)
            for q in wr1b:
                if q["k"] == 1:
                    aggregate_half(A_GAT1A)
                    weights(A_GAT1B)
                if q["k"] == 2:
                    aggregate_half(A_GAT1B)
                wide_product(q, 4 * BANK)
            for half_at in range(2):
                for i in range(NT):
                    pe.wait_ge(h1_done, NT * half_at + i + 1)
                    for k in range(half_at * KH // 2, (half_at + 1) * KH // 2):
                        at = H1T_AT[k // 2] + k % 2 * N + i * P
                        last = pe.transpose(ps[:, at:at + P], z[:, i * HC + k * P:i * HC + (k + 1) * P], ident[:, :])
                        if i == NT - 1 and k % 2 == 1:
                            last.then_inc(h1T_ps, 1)
                for q in plan[4 * KD + half_at * KH // 2:4 * KD + (half_at + 1) * KH // 2]:
                    if q["k"] % 2 == 0:
                        pe.wait_ge(h1T_lo_done, q["k"] // 2 + 1)
                    narrow_product(q, 0)
            for q in plan[4 * KD + KH:]:
                if q["k"] == 2:
                    scores(A_GAT2)
                if q["k"] == 4:
                    weights(A_GAT2)
                if q["k"] == 5:
                    aggregate(A_GAT2)
                narrow_product(q, 3 * BANK)

        @block.vector
        def _(dve):
            def input_lo(b):
                dve.wait_ge(xT_hi_done, b + 1)
                dve.tensor_tensor(xT_lo[:, 2 * b:2 * b + 2, :].rearrange("p k n -> p (k n)"),
                                  ps[:, (5 + b) * BANK:(6 + b) * BANK],
                                  xT_hi[:, 2 * b:2 * b + 2, :].rearrange("p k n -> p (k n)").bitcast(F32),
                                  ALU.subtract).then_inc(xT_lo_done, 1)

            dve.wait_ge(edges_loaded, 32)
            dve.wait_ge(iota_ready, 1)
            dve.tensor_copy(iota[:, :], iota_i).then_inc(edges_cast, 1)
            dve.tensor_copy(edges_f[:, :, :], edges[:, :, :]).then_inc(edges_cast, 1)
            for b in range(3):
                input_lo(b)
            dve.wait_ge(b1_ps, 1)
            dve.tensor_copy(b1_cols[:, :], ps[:, 3 * BANK:3 * BANK + H0 * KD]).then_inc(b1_ready, 1)
            for c in range(POOL_CH, CH):
                split_lo(dve, 0, c)
            dve.wait_ge(edges_cast, 2)
            for t in range(ET):
                for which in range(2):
                    dve.tensor_scalar(hot(t, which), iota[:, :], edges_f[:, which, t:t + 1], None,
                                      ALU.is_equal).then_inc(hot_done, 1)

            def dots(a, t, half_at, done):
                n = heads_of(a)
                w, row = (C1, HC) if n > 1 else (D, D)
                junk = (e1, e2)[half_at][:].rearrange("p a b c -> p (a b c)")
                for i in range(NT):
                    if half_at == 0:
                        dve.wait_ge(hs_done, 2 * a + i + 1)
                    for k in range(first_head(a), first_head(a) + n):
                        at = (k * NT + i) * w if n > 1 else i * D
                        dve.tensor_tensor_reduce(junk[:, at:at + w],
                                                 feat(hs, a, i)[:, (k - first_head(a)) * w:(k - first_head(a) + 1) * w],
                                                 att[:, half_at * row + k * w:half_at * row + (k + 1) * w],
                                                 1.0, 0.0, ALU.mult, ALU.add, t[:, 2 * k + i:2 * k + i + 1])\
                           .then_inc(done, 1)

            def both_dots(a):
                pairs = a + 1 if not isinstance(a, int) or a < A_GAT1B else a
                dve.wait_ge(att_loaded, 32 * pairs)
                dots(a, a_s, 0, a_src_done)
                dots(a, a_d, 1, a_dst_done)

            def maxima(a):
                upto = before(a) + 2 * heads_of(a)
                first = first_head(a)
                small = slice(2 * first, 2 * (first + heads_of(a)))
                dve.wait_ge(a_dst_done, upto)
                dve.wait_ge(scores_bc, a + 1)
                dve.tensor_scalar(a_d2[:, small], a_d[:, small], SLOPE, None, ALU.mult).then_inc(slope_done, 1)
                for k in range(heads_of(a)):
                    for i in range(NT):
                        c = 2 * (first + k) + i
                        dve.tensor_tensor_reduce(am[:, first + k, i, :], ps[:, s_at(a, k):s_at(a, k) + N],
                                                 far[:, i, :], 1.0, -3.0e38, ALU.add, ALU.max, mx[:, c:c + 1])\
                           .then_inc(masked, 1)
                dve.wait_ge(masked, upto)
                dve.tensor_tensor(zc[:, small], mx[:, small], a_d[:, small], ALU.add).then_inc(top_done, 1)
                dve.wait_ge(top_done, a + 1)
                dve.scalar_tensor_tensor(mm[:, small], zc[:, small], SLOPE, zc[:, small], ALU.mult, ALU.max)\
                   .then_inc(m_done, 1)
                dve.wait_ge(m_done, a + 1)
                dve.tensor_tensor(bias1[:, small], a_d[:, small], mm[:, small], ALU.subtract).then_inc(bias_done, 1)
                dve.tensor_tensor(bias2[:, small], a_d2[:, small], mm[:, small], ALU.subtract).then_inc(bias_done, 1)

            def normalise(a):
                for k in range(heads_of(a)):
                    g = first_head(a) + k
                    for i in range(NT):
                        dve.wait_ge(exps_done, 2 * before(a) + 4 * k + 2 * (i + 1))
                        dve.tensor_tensor(e1[:, g, i, :], e1[:, g, i, :], e2[:, g, i, :], ALU.max)\
                           .then_inc(emax_done, 1)
                    for i in range(NT):
                        c = 2 * g + i
                        dve.wait_ge(emax_done, before(a) + 2 * k + i + 1)
                        dve.scalar_tensor_tensor(e2[:, g, i, :], e1[:, g, i, :], 1.0, counts[:, i, :], ALU.mult,
                                                 ALU.mult, accum_out=zsum[:, c:c + 1]).then_inc(p_done, 1)
                if scaled_late(a):
                    return
                inverse_sums(a)
                dve.wait_ge(rz_done, a + 1)
                for i in range(NT):
                    dve.tensor_scalar(am[:, 0, i, :], e2[:, 0, i, :], rz[:, i:i + 1], None,
                                      ALU.mult).then_inc(norm_done, 1)

            def inverse_sums(a):
                dve.wait_ge(p_done, before(a) + 2 * heads_of(a))
                small = slice(2 * first_head(a), 2 * (first_head(a) + heads_of(a)))
                dve.reciprocal(rz[:, small], zsum[:, small]).then_inc(rz_done, 1)

            def weights_lo(a):
                for k in range(heads_of(a)):
                    dve.wait_ge(pT_hi_done, heads_before(a) + k + 1)
                    at = pT_at(a, k)
                    g = first_head(a) + k
                    dve.tensor_tensor(pT_lo[:, g, :, :].rearrange("p j n -> p (j n)"), ps[:, at:at + 2 * N],
                                      pT_hi[:, g, :, :].rearrange("p j n -> p (j n)").bitcast(F32),
                                      ALU.subtract).then_inc(pT_lo_done, 1)

            def elu(h):
                for q in range(3):
                    pair = z[:, 2 * q * N:(2 * q + 2) * N]
                    dve.wait_ge(elu_exp, 6 * h + 2 * q + 2)
                    dve.tensor_scalar(pair, pair, 1.0, -1.0, ALU.min, ALU.add).then_inc(elu_neg, 1)
                    dve.wait_ge(elu_neg, 3 * h + q + 1)
                    for c in range(2):
                        t = 2 * q + c
                        dve.scalar_tensor_tensor(z[:, t * N:(t + 1) * N],
                                                 ps[:, elu_at(h, q) + c * N:elu_at(h, q) + (c + 1) * N],
                                                 b1_cols[:, bass.ds(KD * h + t, 1)], z[:, t * N:(t + 1) * N],
                                                 ALU.add, ALU.max).then_inc(z_done, 1)
                    if q >= 1:
                        elu_lo(h, q - 1)
                elu_lo(h, 2)

            def elu_lo(h, q):
                dve.wait_ge(z_hi_done, 3 * h + q + 1)
                hi = zT_hi[:, 2 * q:2 * q + 2, :].rearrange("p k n -> p (k n)")
                dve.tensor_tensor(zT_lo[:, 2 * q:2 * q + 2, :].rearrange("p k n -> p (k n)"),
                                  z[:, 2 * q * N:(2 * q + 2) * N], hi.bitcast(F32), ALU.subtract)\
                   .then_inc(z_lo_done, 1)

            both_dots(0)
            for c in range(POOL_CH, CH):
                split_lo(dve, 1, c)
            for i in range(NT):
                dve.wait_ge(counted, i + 1)
                dve.tensor_copy(counts[:, i, :], ps[:, (6 + i) * BANK:(6 + i) * BANK + N]).then_inc(counts_copied, 1)
            dve.wait_ge(counts_copied, NT)
            for i in range(NT):
                loops = counts[:, i, i * P:(i + 1) * P]
                dve.tensor_tensor(loops, loops, ident[:, :], ALU.add).then_inc(counts_done, 1)
            dve.wait_ge(counts_done, NT)
            dve.tensor_scalar(far[:, :, :], counts[:, :, :], 0.0, FAR, ALU.is_equal, ALU.mult).then_inc(far_done, 1)
            dve.wait_ge(far_done, 1)

            def softmax_and_elu(h, phase=None):
                both_dots(h)
                maxima(h)
                if phase is not None:
                    split_lo(dve, phase, CH - 1)
                normalise(h)
                weights_lo(h)
                for c in range(POOL_CH, CH):
                    split_lo(dve, 2 * h + 1, c)
                elu(h)

            maxima(0)
            normalise(0)
            weights_lo(0)
            for c in range(POOL_CH, CH):
                split_lo(dve, 2, c)
            elu(0)
            softmax_and_elu(1)
            with dve.Fori(2, H0) as h:
                split_lo(dve, 2 * h, POOL_CH)
                softmax_and_elu(h, phase=2 * h)

            def layer_mean(n, i, parts):
                dve.wait_ge(stats_done, parts)
                dve.bn_aggr(mv[:, i, :], stats[:, i, :, :]).then_inc(aggr_done, 1)
                dve.wait_ge(aggr_done, NT * n + i + 1)
                dve.tensor_scalar(ve[:, i:i + 1], mv[:, i, 1:2], EPS, None, ALU.add).then_inc(ve_done, 1)

            def layer_stats(n, i, t, width):
                part = width // 2
                for s in range(2):
                    dve.bn_stats(stats[:, i, s, :], t[:, s * part:(s + 1) * part]).then_inc(stats_done, 1)
                layer_mean(n, i, 2 * (NT * n + i + 1))

            mine = [q for q in plan if q["who"] == "dve"]
            both_dots(A_CONV2)
            maxima(A_CONV2)
            normalise(A_CONV2)
            weights_lo(A_CONV2)
            inverse_sums(A_CONV2)
            for q in mine[:3]:
                split_lo1(dve, q)
            y = [z[:, i * D:(i + 1) * D] for i in range(NT)]
            dve.wait_ge(xb_done, NT)
            dve.wait_ge(rz_done, A_CONV2 + 1)
            for i in range(NT):
                dve.wait_ge(nat_done, i + 1)
                dve.scalar_tensor_tensor(y[i], ps[:, NAT_AT[i]:NAT_AT[i] + D], rz[:, i:i + 1], x_sb[:, i, :],
                                         ALU.mult, ALU.add).then_inc(biased, 1)
                dve.wait_ge(biased, i + 1)
                layer_stats(0, i, y[i], D)
            for i in range(NT):
                dve.wait_ge(rstd_done, i + 1)
                dve.tensor_scalar(x_sb[:, i, :], y[i], mv[:, i, 0:1], rstd[:, i:i + 1], ALU.subtract, ALU.mult)\
                   .then_inc(x1_done, 1)
            for b in range(KD // 2):
                dve.wait_ge(x1T_hi_done, b + 1)
                hi = xT_hi[:, 2 * b:2 * b + 2, :].rearrange("p k n -> p (k n)")
                dve.tensor_tensor(xT_lo[:, 2 * b:2 * b + 2, :].rearrange("p k n -> p (k n)"),
                                  ps[:, X1T_AT[b]:X1T_AT[b] + 2 * N], hi.bitcast(F32), ALU.subtract)\
                   .then_inc(x1T_lo_done, 1)
            for q in mine[3:6]:
                split_lo1(dve, q)
            both_dots(A_GAT1A)
            maxima(A_GAT1A)
            normalise(A_GAT1A)
            both_dots(A_GAT1B)
            maxima(A_GAT1B)
            weights_lo(A_GAT1A)
            inverse_sums(A_GAT1A)
            normalise(A_GAT1B)
            dve.wait_ge(rows_loaded, 16 * 8)

            def columns(half_at):
                return slice(half_at * HW, (half_at + 1) * HW)

            def residual(half_at):
                dve.wait_ge(chunk_used, plan[(3 + half_at) * KD - 1]["n"] + 1)
                dve.wait_ge(h_lo_done, 2 * (A_GAT1A + half_at) + 2)
                for i in range(NT):
                    at = 4 * BANK + i * HC + half_at * HW
                    dve.tensor_tensor(hs[:, at - 4 * BANK:at - 4 * BANK + HW], ps[:, at:at + HW],
                                      rows_hc[:, 3, columns(half_at)], ALU.add).then_inc(r_added, 1)

            y1 = [z[:, i * HC:(i + 1) * HC] for i in range(NT)]

            def biased_half(half_at, i):
                a = A_GAT1A + half_at
                dve.wait_ge(nat_done, 2 * NT + i + 1 - NT * (1 - half_at))
                for k in range(first_head(a), first_head(a) + HH):
                    dve.scalar_tensor_tensor(y1[i][:, k * C1:(k + 1) * C1],
                                             ps[:, i * HC + k * C1:i * HC + (k + 1) * C1],
                                             rz[:, 2 * k + i:2 * k + i + 1], rows_hc[:, 0, k * C1:(k + 1) * C1],
                                             ALU.mult, ALU.add).then_inc(biased, 1)
                dve.wait_ge(biased, NT + HH * (NT * half_at + i + 1))
                dve.bn_stats(stats[:, i, half_at, :], y1[i][:, columns(half_at)]).then_inc(stats_done, 1)

            dve.wait_ge(rz_done, A_GAT1A + 1)
            biased_half(0, 0)
            biased_half(0, 1)
            weights_lo(A_GAT1B)
            inverse_sums(A_GAT1B)
            residual(0)
            dve.wait_ge(rz_done, A_GAT1B + 1)
            for i in range(NT):
                biased_half(1, i)
                layer_mean(1, i, 3 * NT + i + 1)

            def h1_half(half_at):
                cols = columns(half_at)
                for i in range(NT):
                    dve.scalar_tensor_tensor(y1[i][:, cols], y1[i][:, cols], mv[:, i, 0:1], rows_hc[:, 1, cols],
                                             ALU.subtract, ALU.mult).then_inc(norm1, 1)
                for i in range(NT):
                    dve.wait_ge(norm1, NT * half_at + i + 1)
                    dve.wait_ge(rstd_done, NT + i + 1)
                    dve.scalar_tensor_tensor(y1[i][:, cols], y1[i][:, cols], rstd[:, i:i + 1],
                                             rows_hc[:, 2, cols], ALU.mult, ALU.add).then_inc(norm2, 1)
                dve.wait_ge(r_added, NT * (half_at + 1))
                for i in range(NT):
                    dve.wait_ge(norm2, NT * half_at + i + 1)
                    dve.scalar_tensor_tensor(y1[i][:, cols], y1[i][:, cols], 0.0,
                                             hs[:, i * HC + half_at * HW:i * HC + (half_at + 1) * HW],
                                             ALU.max, ALU.add).then_inc(h1_done, 1)

            def h1_lo(b):
                dve.wait_ge(h1T_hi_done, b + 1)
                hi = zT_hi[:, 2 * b:2 * b + 2, :].rearrange("p k n -> p (k n)")
                dve.tensor_tensor(zT_lo[:, 2 * b:2 * b + 2, :].rearrange("p k n -> p (k n)"),
                                  ps[:, H1T_AT[b]:H1T_AT[b] + 2 * N], hi.bitcast(F32), ALU.subtract)\
                   .then_inc(h1T_lo_done, 1)

            h1_half(0)
            h1_lo(0)
            h1_lo(1)
            residual(1)
            h1_half(1)
            split_lo1(dve, mine[6])
            h1_lo(2)
            h1_lo(3)
            split_lo1(dve, mine[7])
            shift = [rows_hc[:, i, 0:D] for i in range(NT)]
            for i in range(NT):
                dve.tensor_tensor(shift[i], x_sb[:, i, :], rows_d[:, 2, :], ALU.add).then_inc(shifted, 1)
            dve.wait_ge(shifted, NT)
            for i in range(NT):
                dve.tensor_tensor(shift[i], shift[i], rows_d[:, 3, :], ALU.add).then_inc(shifted, 1)
            for q in mine[8:]:
                split_lo1(dve, q)
            both_dots(A_GAT2)
            maxima(A_GAT2)
            normalise(A_GAT2)
            weights_lo(A_GAT2)
            inverse_sums(A_GAT2)
            dve.wait_ge(shifted, 2 * NT)
            dve.wait_ge(rz_done, A_GAT2 + 1)
            for i in range(NT):
                dve.wait_ge(nat_done, 3 * NT + i + 1)
                dve.scalar_tensor_tensor(y[i], ps[:, NAT_AT[i]:NAT_AT[i] + D], rz[:, i:i + 1], rows_d[:, 0, :],
                                         ALU.mult, ALU.add).then_inc(biased, 1)
                dve.wait_ge(biased, NT + 2 * H1 + i + 1)
                layer_stats(2, i, y[i], D)
            for i in range(NT):
                dve.scalar_tensor_tensor(y[i], y[i], mv[:, i, 0:1], rows_d[:, 1, :], ALU.subtract, ALU.mult)\
                   .then_inc(norm1, 1)
            for i in range(NT):
                dve.wait_ge(norm1, 2 * NT + i + 1)
                dve.wait_ge(rstd_done, 2 * NT + i + 1)
                dve.scalar_tensor_tensor(y[i], y[i], rstd[:, i:i + 1], shift[i], ALU.mult, ALU.add)\
                   .then_inc(norm2, 1)
            dve.wait_ge(chunk_used, plan[-1]["n"] + 1)
            for i in range(NT):
                dve.wait_ge(norm2, 2 * NT + i + 1)
                dve.tensor_tensor(y[i], ps[:, 3 * BANK + i * D:3 * BANK + (i + 1) * D], y[i], ALU.add)\
                   .then_inc(r2_added, 1)
                dve.wait_ge(r2_added, i + 1)
                layer_stats(3, i, y[i], D)
            for i in range(NT):
                dve.wait_ge(rstd_done, 3 * NT + i + 1)
                dve.tensor_scalar(x_sb[:, i, :], y[i], mv[:, i, 0:1], rstd[:, i:i + 1], ALU.subtract, ALU.mult)\
                   .then_inc(out_ready, 1)


INPUTS = ["x", "src", "dst"] \
    + ["L0_gnn_" + n for n in ("W1", "a_src1", "a_dst1", "b1", "W2", "a_src2", "a_dst2", "b2")] \
    + ["L1_gnn_" + n for n in ("W1", "a_src1", "a_dst1", "b1", "g1", "be1", "Wr1", "br1",
                               "W2", "a_src2", "a_dst2", "b2", "g2", "be2", "Wr2", "br2")]


def kernel(**inputs):
    import numpy as np
    import concourse.bacc as bacc
    from concourse.bass_utils import run_bass_kernel_spmd

    nc = bacc.Bacc("TRN2", target_bir_lowering=False, num_devices=1)
    arrays, args = {}, []
    for name in INPUTS:
        a = np.ascontiguousarray(inputs[name])
        arrays[f"in_{name}"] = a
        args.append(nc.dram_tensor(f"in_{name}", a.shape, mybir.dt.from_np(a.dtype), kind="ExternalInput").ap())
    out = nc.dram_tensor("out", (N, D), F32, kind="ExternalOutput").ap()
    build_gnn(nc, *args, out)
    r = run_bass_kernel_spmd(nc, [arrays], core_ids=[0])
    return r.results[0]["out"]
```

```python
from contextlib import ExitStack

import concourse.bass as bass
from concourse import mybir

ALU = mybir.AluOpType
ACT = mybir.ActivationFunctionType
F32 = mybir.dt.float32
F32R = mybir.dt.float32r
BF16 = mybir.dt.bfloat16
I32 = mybir.dt.int32

P = 128
N = 256
NT = N // P
D = 768
KD = D // P
H0 = 8
H1, C1 = 4, 256
HC = H1 * C1
KH = HC // P
E = 4096
ET = E // P
BANK = 512
SLOPE = 0.2
EPS = 1e-5
FAR = -1.0e30

CH = KD
RG = 3
POOL_CH = 4
DVE_CH = CH - POOL_CH
FIRST = 1
PHASES = 2 * H0

A_CONV2, A_GAT1A, A_GAT1B, A_GAT2 = H0, H0 + 1, H0 + 2, H0 + 3
HH = H1 // 2
HW = HH * C1


def block1_plan():
    plan = []
    pool, dve = POOL_CH * PHASES - FIRST, DVE_CH * PHASES + FIRST
    loads = [PHASES] * RG
    free_at = [("pool", pool - 2), ("pool", pool), ("dve", dve)]
    used0 = CH * PHASES

    def group(what, part, k, width, who, slots, used):
        nonlocal pool, dve
        g = group.n % RG
        group.n += 1
        loads[g] += 1
        free = free_at[g]
        for m, (slot, need) in enumerate(zip(slots, used)):
            if who == "dve":
                dve += 1
            else:
                pool += 1
            plan.append(dict(what=what, part=part, k=k + m, width=width, raw_group=g, raw_at=m * width,
                             first=m == 0, chunks=len(slots), free=free, full=16 * loads[g],
                             ring_at=slot * width, used=need, who=who,
                             lo=dve if who == "dve" else pool, n=used0 + len(plan)))
        free_at[g] = (who, dve if who == "dve" else pool)

    group.n = 0
    slots_w = CH * D // HW
    wide = 4 * KD
    for i in range(0, wide, 3):
        slots, needs = [], []
        for j in range(i, i + 3):
            slots.append(j % slots_w)
            if j < slots_w:
                needs.append(used0 - CH + (HW * (j + 1) - 1) // D + 1)
            else:
                needs.append(used0 + j - slots_w + 1)
        half, k = divmod(i, KD)
        group("W1" if half < 2 else "Wr1", half % 2, k, HW, "dve" if i in (6, 9) else "pool", slots, needs)
    for i in range(0, 2 * KH, 2):
        slots, needs = [], []
        for j in (i, i + 1):
            slot = (j + 4) % CH
            slots.append(slot)
            if j < CH:
                lo, hi = D * slot // HW, (D * (slot + 1) - 1) // HW
                needs.append(used0 + max(max(m for m in range(wide) if m % slots_w == v)
                                         for v in range(lo, hi + 1)) + 1)
            else:
                needs.append(used0 + wide + j - CH + 1)
        group("W2" if i < KH else "Wr2", 0, i % KH, D, "dve" if i in (6, 12) else "pool", slots, needs)
    return plan


def build_gnn(nc, x, src, dst, b0_W1, b0_as1, b0_ad1, b0_b1, b0_W2, b0_as2, b0_ad2, b0_b2,
              b1_W1, b1_as1, b1_ad1, b1_b1, b1_g1, b1_be1, b1_Wr1, b1_br1,
              b1_W2, b1_as2, b1_ad2, b1_b2, b1_g2, b1_be2, b1_Wr2, b1_br2, out):
    plan = block1_plan()
    wide_chunks = 2 * KD
    ctx = ExitStack()
    with ctx:
        def sb(name, shape, dt=F32):
            return ctx.enter_context(nc.sbuf_tensor(name, shape, dt))

        def sem(name):
            return ctx.enter_context(nc.semaphore(name))

        x_sb = sb("x_sb", [P, NT, D])
        xT_hi = sb("xT_hi", [P, KD, N], F32R)
        xT_lo = sb("xT_lo", [P, KD, N], F32R)
        counts = sb("counts", [P, NT, N])
        far = sb("far", [P, NT, N])
        ident = sb("ident", [P, P])
        zeros = sb("zeros", [P, BANK], BF16)
        iota = sb("iota", [P, N], BF16)
        edges = sb("edges", [P, 2, ET], I32)
        edges_f = sb("edges_f", [P, 2, ET])
        raw = sb("raw", [P, RG, 2 * D])
        ring_hi = sb("ring_hi", [P, CH * D], F32R)
        ring_lo = sb("ring_lo", [P, CH * D], F32R)
        att = sb("att", [P, 2 * HC])
        hs = sb("hs", [P, NT * HC])
        h_hi = sb("h_hi", [P, NT * HC], F32R)
        h_lo = sb("h_lo", [P, NT * HC], F32R)
        pT_hi = sb("pT_hi", [P, H1, NT, N], F32R)
        pT_lo = sb("pT_lo", [P, H1, NT, N], F32R)
        zT_hi = sb("zT_hi", [P, KH, N], F32R)
        zT_lo = sb("zT_lo", [P, KH, N], F32R)
        z = sb("z", [P, KH * N])
        am = sb("am", [P, H1, NT, N])
        e1 = sb("e1", [P, H1, NT, N])
        e2 = sb("e2", [P, H1, NT, N])
        b1_cols = sb("b1_cols", [P, H0 * KD])
        b1_rows = sb("b1_rows", [H0 * KD, P])
        rows_hc = sb("rows_hc", [P, 4, HC])
        rows_d = sb("rows_d", [P, 4, D])
        PAIRS = NT * H1
        a_s = sb("a_s", [P, PAIRS])
        a_d = sb("a_d", [P, PAIRS])
        a_d2 = sb("a_d2", [P, PAIRS])
        mx = sb("mx", [P, PAIRS])
        zc = sb("zc", [P, PAIRS])
        mm = sb("mm", [P, PAIRS])
        bias1 = sb("bias1", [P, PAIRS])
        bias2 = sb("bias2", [P, PAIRS])
        zsum = sb("zsum", [P, PAIRS])
        rz = sb("rz", [P, PAIRS])
        stats = sb("stats", [P, NT, 2, 6])
        mv = sb("mv", [P, NT, 2])
        ve = sb("ve", [P, NT])
        minus_mean = sb("minus_mean", [P, NT])
        offset = sb("offset", [P, NT])
        rstd = sb("rstd", [P, NT])
        half = sb("half", [P, 1])

        hot_homes = [t.bitcast(BF16) for t in (am[:].rearrange("p a b c -> p (a b c)"),
                                               z[:], rows_hc[:, 0:2, :].rearrange("p a c -> p (a c)"),
                                               rows_hc[:, 2:4, :].rearrange("p a c -> p (a c)"))]
        per_home = ET // len(hot_homes)

        def hot(t, which):
            at = ((t % per_home) * 2 + which) * N
            return hot_homes[t // per_home][:, at:at + N]

        iota_i = hs[:, 0:N].bitcast(I32)

        ps = ctx.enter_context(nc.psum_tensor("ps", [P, 8 * BANK], F32))
        PROJ, ACC = 0, 3 * BANK
        S_AT, T_AT = 6 * BANK, 7 * BANK
        NAT_AT = [0, 6 * BANK]
        X1T_AT = [3 * BANK, 5 * BANK]
        X1T_PARTS = [4, KD]
        H1_PART = KH // 2
        ELU_AT = [2 * BANK, 6 * BANK, 7 * BANK]

        raw_full = [sem(f"raw_full{g}") for g in range(RG)]
        hi_done = sem("hi_done")
        lo_by = {"pool": sem("lo_pool"), "dve": sem("lo_dve")}
        chunk_used = sem("chunk_used")
        first_loaded = sem("first_loaded")
        x_loaded = sem("x_loaded")
        b2_loaded = sem("b2_loaded")
        edges_loaded = sem("edges_loaded")
        b1_loaded = sem("b1_loaded")
        rows_loaded = sem("rows_loaded")
        att_loaded = sem("att_loaded")
        half_set = sem("half_set")
        zeros_set = sem("zeros_set")
        consts = sem("consts")
        iota_ready = sem("iota_ready")
        xT_ps = sem("xT_ps")
        xT_hi_done = sem("xT_hi_done")
        xT_lo_done = sem("xT_lo_done")
        edges_cast = sem("edges_cast")
        hot_done = sem("hot_done")
        counted = sem("counted")
        counts_copied = sem("counts_copied")
        counts_done = sem("counts_done")
        far_done = sem("far_done")
        b1_ps = sem("b1_ps")
        b1_ready = sem("b1_ready")
        xb_done = sem("xb_done")
        hs_done = sem("hs_done")
        h_hi_done = sem("h_hi_done")
        h_lo_done = sem("h_lo_done")
        a_src_done = sem("a_src_done")
        a_dst_done = sem("a_dst_done")
        scores_bc = sem("scores_bc")
        masked = sem("masked")
        top_done = sem("top_done")
        m_done = sem("m_done")
        bias_done = sem("bias_done")
        exps_done = sem("exps_done")
        emax_done = sem("emax_done")
        p_done = sem("p_done")
        rz_done = sem("rz_done")
        norm_done = sem("norm_done")
        pT_ps = sem("pT_ps")
        pT_hi_done = sem("pT_hi_done")
        pT_lo_done = sem("pT_lo_done")
        wt_ps = sem("wt_ps")
        wt_hi_done = sem("wt_hi_done")
        wt_lo_done = sem("wt_lo_done")
        agg_done = sem("agg_done")
        elu_exp = sem("elu_exp")
        elu_neg = sem("elu_neg")
        z_done = sem("z_done")
        z_hi_done = sem("z_hi_done")
        z_lo_done = sem("z_lo_done")
        nat_done = sem("nat_done")
        biased = sem("biased")
        stats_done = sem("stats_done")
        aggr_done = sem("aggr_done")
        minus_mean_done = sem("minus_mean_done")
        offset_done = sem("offset_done")
        act_normed = sem("act_normed")
        ve_done = sem("ve_done")
        rstd_done = sem("rstd_done")
        norm1 = sem("norm1")
        norm2 = sem("norm2")
        scaled = sem("scaled")
        x1_done = sem("x1_done")
        tile0_done = sem("tile0_done")
        x1T_ps = sem("x1T_ps")
        x1T_hi_done = sem("x1T_hi_done")
        x1T_lo_done = sem("x1T_lo_done")
        r_added = sem("r_added")
        h1_done = sem("h1_done")
        h1T_ps = sem("h1T_ps")
        h1T_hi_done = sem("h1T_hi_done")
        h1T_lo_done = sem("h1T_lo_done")
        r2_added = sem("r2_added")
        be_added = sem("be_added")
        shifted = sem("shifted")
        out_ready = sem("out_ready")
        stored = sem("stored")

        block = ctx.enter_context(nc.Block())

        FIRST_PHASE = 0

        def slot_hi(c):
            return ring_hi[:, c * D:(c + 1) * D]

        def slot_lo(c):
            return ring_lo[:, c * D:(c + 1) * D]

        def raw_chunk(c):
            return raw[:, c // 2, (c % 2) * D:(c % 2 + 1) * D]

        def split_hi(eng, p, c, reused=True):
            if p is FIRST_PHASE and c == 0:
                eng.wait_ge(first_loaded, 16)
            elif c % 2 == 0 or p is FIRST_PHASE and c == 1:
                eng.wait_ge(raw_full[c // 2], 16 * p + 16)
            if reused:
                eng.wait_ge(chunk_used, CH * p + c - CH + 1)
            eng.activation(slot_hi(c), raw_chunk(c), ACT.Copy).then_inc(hi_done, 1)

        def lo_count(p, c):
            if c < POOL_CH and not (p is FIRST_PHASE and c < FIRST):
                return lo_by["pool"], POOL_CH * p + c + 1 - FIRST
            if c < FIRST:
                return lo_by["dve"], c + 1
            return lo_by["dve"], DVE_CH * p + c - POOL_CH + 1 + FIRST

        def split_lo(eng, p, c):
            eng.wait_ge(hi_done, CH * p + c + 1)
            eng.tensor_tensor(slot_lo(c), raw_chunk(c), slot_hi(c).bitcast(F32), ALU.subtract)\
               .then_inc(lo_count(p, c)[0], 1)

        def split_hi1(eng, q):
            if q["first"]:
                eng.wait_ge(raw_full[q["raw_group"]], q["full"])
            eng.wait_ge(chunk_used, q["used"])
            w = q["width"]
            eng.activation(ring_hi[:, q["ring_at"]:q["ring_at"] + w],
                           raw[:, q["raw_group"], q["raw_at"]:q["raw_at"] + w], ACT.Copy)\
               .then_inc(hi_done, 1)

        def split_lo1(eng, q):
            eng.wait_ge(hi_done, q["n"] + 1)
            w = q["width"]
            eng.tensor_tensor(ring_lo[:, q["ring_at"]:q["ring_at"] + w],
                              raw[:, q["raw_group"], q["raw_at"]:q["raw_at"] + w],
                              ring_hi[:, q["ring_at"]:q["ring_at"] + w].bitcast(F32), ALU.subtract)\
               .then_inc(lo_by[q["who"]], 1)

        def is_gat1(a):
            return isinstance(a, int) and a in (A_GAT1A, A_GAT1B)

        def heads_of(a):
            return HH if is_gat1(a) else 1

        def first_head(a):
            return HH * (a - A_GAT1A) if is_gat1(a) else 0

        def feat(t, a, i):
            if is_gat1(a):
                at = i * HC + (a - A_GAT1A) * HW
                return t[:, at:at + HW]
            return t[:, i * D:(i + 1) * D]

        def source_at(a, i):
            if is_gat1(a):
                at = i * HC + (a - A_GAT1A) * HW
                return ps[:, at:at + HW]
            at = (ACC if isinstance(a, int) and a in (0, A_CONV2) else PROJ) + i * D
            return ps[:, at:at + D]

        def pT_at(a, k):
            return (2 - 2 * k + a - A_GAT1A) * BANK if is_gat1(a) else T_AT

        def s_at(a, k):
            return (a - A_GAT1A) * BANK + k * N if is_gat1(a) else S_AT

        def elu_at(h, q):
            if isinstance(h, int) and h == 0:
                return ELU_AT[(q + 1) % 3]
            return ELU_AT[q]

        def heads_before(a):
            return a if not isinstance(a, int) or a <= A_GAT1A else a + min(a - A_GAT1A, 2) * (HH - 1)

        def before(a):
            return 2 * heads_before(a)

        def x1T_part(t, i, part):
            k0, k1 = 0 if part == 0 else X1T_PARTS[0], X1T_PARTS[part]
            at = X1T_AT[i] + k0 * P
            return (t[:, k0:k1, i * P:(i + 1) * P],
                    ps[:, at:at + (k1 - k0) * P].rearrange("p (k n) -> p k n", n=P))

        def shift(i):
            at = NT * N + i * D
            return am[:].rearrange("p a b c -> p (a b c)")[:, at:at + D]

        def h1T_at(half_at, i):
            return (4 + 2 * i + half_at) * BANK

        def h1T_part(t, half_at, i):
            at = h1T_at(half_at, i)
            return (t[:, half_at * H1_PART:(half_at + 1) * H1_PART, i * P:(i + 1) * P],
                    ps[:, at:at + H1_PART * P].rearrange("p (k n) -> p k n", n=P))

        OUT_HALVES = (slice(0, D // 2), slice(D // 2, D))

        ON_ACT = [(0, 0), (2, 1), (3, 0)]

        def scaled_late(a):
            return isinstance(a, int) and a >= A_CONV2

        WT_AT = [T_AT, 2 * BANK]

        def tiles_before(a):
            return NT if a == A_GAT2 else 0

        def weights_tile(t, i):
            return (t[:, 0, :, i * P:(i + 1) * P],
                    ps[:, WT_AT[i]:WT_AT[i] + N].rearrange("p (j n) -> p j n", n=P))

        def pT_before(a):
            return heads_before(a) - (1 if isinstance(a, int) and a > A_CONV2 else 0)

        PASSES = 3

        def three(hi_a, lo_a, hi_b, lo_b):
            return ((hi_a, hi_b), (hi_a, lo_b), (lo_a, hi_b))

        @block.sync
        def _(sp):
            w1 = b0_W1.rearrange("(k p) (h c) -> p k h c", p=P, c=D)
            w2 = b0_W2.rearrange("(h k p) c -> p h k c", p=P, k=KD)

            def load(p, g, view):
                dst_ap = raw[:, g, :].rearrange("p (k c) -> p k c", k=2)
                sp.dma_start(dst_ap, view).then_inc(raw_full[g], 16)

            def load_phase(p, view):
                for g in range(RG):
                    if g < RG - 1:
                        sp.wait_ge(lo_by["pool"], POOL_CH * p - POOL_CH + 2 * (g + 1) - FIRST)
                    else:
                        sp.wait_ge(lo_by["dve"], DVE_CH * p + FIRST)
                    load(p, g, view(g))

            def w1_of(h):
                return lambda g: w1[:, 2 * g:2 * g + 2, bass.ds(h, 1), :].rearrange("p k h c -> p k (h c)")

            def w2_of(h):
                return lambda g: w2[:, bass.ds(h, 1), 2 * g:2 * g + 2, :].rearrange("p h k c -> p (h k) c")

            sp.dma_start(x_sb[:, :, :], x.rearrange("(t p) c -> p t c", p=P)).then_inc(x_loaded, 16)
            sp.dma_start(raw[:, 0, 0:D], w1[:, 0, 0, :]).then_inc(first_loaded, 16)
            sp.dma_start(raw[:, 0, D:2 * D], w1[:, 1, 0, :]).then_inc(raw_full[0], 16)
            for g in range(1, RG):
                load(0, g, w1_of(0)(g))
            sp.wait_ge(lo_by["dve"], FIRST)
            load_phase(1, w1_of(1))
            load_phase(2, w2_of(0))
            sp.wait_ge(counted, NT)
            for n, v in enumerate((b1_b1, b1_g1, b1_be1, b1_br1)):
                sp.dma_start(rows_hc[:, n, :], v.partition_broadcast(P)).then_inc(rows_loaded, 16)
            for n, v in enumerate((b1_b2, b1_g2, b1_be2)):
                sp.dma_start(rows_d[:, n, :], v.partition_broadcast(P)).then_inc(rows_loaded, 16)
            with sp.Fori(2, H0) as h:
                load_phase(2 * h - 1, w1_of(h))
                load_phase(2 * h, w2_of(h - 1))
            load_phase(PHASES - 1, w2_of(H0 - 1))
            views = {"W1": b1_W1, "Wr1": b1_Wr1, "W2": b1_W2, "Wr2": b1_Wr2}
            for q in plan:
                if not q["first"]:
                    continue
                who, count = q["free"]
                sp.wait_ge(lo_by[who], count)
                at = q["part"] * q["width"]
                view = views[q["what"]].rearrange("(k p) c -> p k c", p=P)[:, q["k"]:q["k"] + q["chunks"],
                                                                          at:at + q["width"]]
                width = q["chunks"] * q["width"]
                sp.dma_start(raw[:, q["raw_group"], 0:width].rearrange("p (k c) -> p k c", k=q["chunks"]),
                             view).then_inc(raw_full[q["raw_group"]], 16)
            sp.wait_ge(act_normed, len(ON_ACT))
            sp.dma_start(out[0:P, :], x_sb[:, 0, :]).then_inc(stored, 16)
            for n, cols in enumerate(OUT_HALVES):
                sp.wait_ge(out_ready, n + 1)
                sp.dma_start(out[P:N, cols], x_sb[:, 1, cols]).then_inc(stored, 16)
            sp.wait_ge(stored, 16 * 3)

        @block.gpsimd
        def _(pool):
            pool.memset(half[:, :], -0.5).then_inc(half_set, 1)
            pool.memset(zeros[:, :], 0.0).then_inc(zeros_set, 1)
            pool.memset(ident[:, :], 0.0).then_inc(consts, 1)
            pool.wait_ge(consts, 1)
            pool.affine_select(out=ident[:, :], in_=ident[:, :], compare_op=ALU.not_equal, fill=1.0,
                               base=0, pattern=[[-1, P]], channel_multiplier=1).then_inc(consts, 1)
            pool.iota(iota_i, pattern=[[1, N]], base=0, channel_multiplier=0).then_inc(iota_ready, 1)
            for c in range(FIRST, POOL_CH):
                split_lo(pool, FIRST_PHASE, c)

            def features_lo(a):
                for i in range(NT):
                    pool.wait_ge(h_hi_done, 2 * a + i + 1)
                    pool.tensor_tensor(feat(h_lo, a, i), feat(hs, a, i), feat(h_hi, a, i).bitcast(F32),
                                       ALU.subtract).then_inc(h_lo_done, 1)

            def phase_lo(p):
                for c in range(POOL_CH):
                    split_lo(pool, p, c)

            def head(h):
                phase_lo(2 * h)
                features_lo(h)
                phase_lo(2 * h + 1)

            phase_lo(1)
            features_lo(0)
            pool.wait_ge(b2_loaded, 16)
            pool.wait_ge(xT_ps, 3)
            for i in range(NT):
                pool.tensor_tensor(x_sb[:, i, :], x_sb[:, i, :], rows_d[:, 3, :], ALU.add).then_inc(xb_done, 1)
            with pool.Fori(1, H0) as h:
                head(h)

            def inverse_root(n, i):
                pool.wait_ge(ve_done, NT * n + i + 1)
                pool.tensor_tensor(rstd[:, i:i + 1], ve[:, i:i + 1], half[:, :], ALU.pow).then_inc(rstd_done, 1)
                if (n, i) in ON_ACT:
                    pool.wait_ge(rstd_done, NT * n + i + 1)
                    pool.wait_ge(minus_mean_done, ON_ACT.index((n, i)) + 1)
                    pool.tensor_tensor(offset[:, i:i + 1], minus_mean[:, i:i + 1], rstd[:, i:i + 1], ALU.mult)\
                        .then_inc(offset_done, 1)

            mine = [q for q in plan if q["who"] == "pool"]
            wide = [q for q in mine if q["width"] == HW]
            narrow = [q for q in mine if q["width"] == D]
            features_lo(A_CONV2)
            for q in wide[:6]:
                split_lo1(pool, q)
            for i in range(NT):
                inverse_root(0, i)
            for q in wide[6:9]:
                split_lo1(pool, q)
            features_lo(A_GAT1A)
            for q in wide[9:12]:
                split_lo1(pool, q)
            features_lo(A_GAT1B)
            for q in wide[12:]:
                split_lo1(pool, q)
            for q in narrow[:3]:
                split_lo1(pool, q)
            for i in range(NT):
                inverse_root(1, i)
            for q in narrow[3:6]:
                split_lo1(pool, q)
            pool.wait_ge(rows_loaded, 16 * 8)
            pool.tensor_tensor(rows_d[:, 2, :], rows_d[:, 2, :], rows_d[:, 3, :], ALU.add).then_inc(be_added, 1)
            pool.wait_ge(be_added, 1)
            pool.wait_ge(x1_done, 1)
            pool.wait_ge(act_normed, 1)
            pool.wait_ge(exps_done, 2 * before(A_GAT2))
            for i in range(NT):
                pool.tensor_tensor(shift(i), x_sb[:, i, :], rows_d[:, 2, :], ALU.add).then_inc(shifted, 1)
            for q in narrow[6:10]:
                split_lo1(pool, q)
            features_lo(A_GAT2)
            for q in narrow[10:]:
                split_lo1(pool, q)
            for i in range(NT):
                inverse_root(2, i)
            y1 = z[:, D:2 * D]
            pool.wait_ge(act_normed, ON_ACT.index((2, 1)) + 1)
            pool.tensor_tensor(y1, y1, rows_d[:, 1, :], ALU.mult).then_inc(scaled, 1)
            for i in range(NT):
                inverse_root(3, i)

        @block.scalar
        def _(act):
            def load_att(n, a_src, a_dst, width, reused=True):
                if reused:
                    act.wait_ge(a_dst_done, 2 * n)
                for half_at, v in ((0, a_src), (1, a_dst)):
                    act.dma_start(att[:, half_at * width:(half_at + 1) * width], v.partition_broadcast(P))\
                       .then_inc(att_loaded, 16)

            def att_row(t, h):
                return t[bass.ds(h, 1), :]

            act.wait_ge(half_set, 1)
            act.activation(rstd[:, 0:1], half[:, :], ACT.Exp)
            act.dma_start(edges[:, 0, :], src.rearrange("(p t) -> p t", p=P)).then_inc(edges_loaded, 16)
            act.dma_start(edges[:, 1, :], dst.rearrange("(p t) -> p t", p=P)).then_inc(edges_loaded, 16)
            act.dma_start(b1_rows[:, :], b0_b1.rearrange("(t p) -> t p", p=P)).then_inc(b1_loaded, 16)
            load_att(0, b0_as1[0:1, :], b0_ad1[0:1, :], D, reused=False)

            for b in range(3):
                act.wait_ge(xT_ps, b + 1)
                act.activation(xT_hi[:, 2 * b:2 * b + 2, :].rearrange("p k n -> p (k n)"),
                               ps[:, (5 + b) * BANK:(6 + b) * BANK], ACT.Copy).then_inc(xT_hi_done, 1)
                if b == 0:
                    split_hi(act, FIRST_PHASE, 0, reused=False)
            for c in range(1, CH):
                split_hi(act, FIRST_PHASE, c, reused=False)
            act.dma_start(rows_d[:, 3, :], b0_b2.partition_broadcast(P)).then_inc(b2_loaded, 16)

            def features_copy(a, chunks, tile0=None, tiles=range(NT)):
                for i in tiles:
                    if i == 0 and tile0 is not None:
                        act.wait_ge(tile0_done, tile0)
                    elif i == 0 or tile0 is not None:
                        act.wait_ge(chunk_used, chunks)
                    act.activation(feat(hs, a, i), source_at(a, i), ACT.Copy).then_inc(hs_done, 1)

            def features_hi(a, tiles=range(NT)):
                for i in tiles:
                    act.wait_ge(hs_done, 2 * a + i + 1)
                    act.activation(feat(h_hi, a, i), feat(hs, a, i), ACT.Copy).then_inc(h_hi_done, 1)

            def layer_norm(n, i, to, t):
                act.wait_ge(offset_done, ON_ACT.index((n, i)) + 1)
                act.activation(to, t, ACT.Identity, bias=offset[:, i:i + 1], scale=rstd[:, i:i + 1])\
                   .then_inc(act_normed, 1)

            y = [z[:, i * D:(i + 1) * D] for i in range(NT)]

            def exps(a):
                act.wait_ge(bias_done, 2 * a + 2)
                for k in range(first_head(a), first_head(a) + heads_of(a)):
                    for i in range(NT):
                        c = 2 * k + i
                        act.activation(e1[:, k, i, :], am[:, k, i, :], ACT.Exp, bias=bias1[:, c:c + 1])\
                           .then_inc(exps_done, 1)
                        act.activation(e2[:, k, i, :], am[:, k, i, :], ACT.Exp, bias=bias2[:, c:c + 1],
                                       scale=SLOPE).then_inc(exps_done, 1)

            def weights_hi(a):
                for k in range(heads_of(a)):
                    act.wait_ge(pT_ps, pT_before(a) + k + 1)
                    at = pT_at(a, k)
                    act.activation(pT_hi[:, first_head(a) + k, :, :].rearrange("p j n -> p (j n)"),
                                   ps[:, at:at + 2 * N], ACT.Copy).then_inc(pT_hi_done, 1)

            def weights_tiles_hi(a):
                for i in range(NT):
                    act.wait_ge(wt_ps, tiles_before(a) + i + 1)
                    act.activation(*weights_tile(pT_hi, i), ACT.Copy).then_inc(wt_hi_done, 1)

            def elu(h, first=False):
                for q in range(3):
                    act.wait_ge(agg_done, 3 * h + q + 1)
                    if not first:
                        act.wait_ge(z_lo_done, 3 * h + q - 2)
                    for c in range(2):
                        t = 2 * q + c
                        at = elu_at(h, q) + c * N
                        act.activation(z[:, t * N:(t + 1) * N], ps[:, at:at + N], ACT.Exp,
                                       bias=b1_cols[:, bass.ds(KD * h + t, 1)]).then_inc(elu_exp, 1)
                    if q >= 1:
                        elu_hi(h, q - 1)
                elu_hi(h, 2)

            def elu_hi(h, q):
                act.wait_ge(z_done, 6 * h + 2 * q + 2)
                act.activation(zT_hi[:, 2 * q:2 * q + 2, :].rearrange("p k n -> p (k n)"),
                               z[:, 2 * q * N:(2 * q + 2) * N], ACT.Copy).then_inc(z_hi_done, 1)

            def att_for(h, last=False):
                if last:
                    load_att(h, b0_as2[0:1, :], b0_ad2[0:1, :], D)
                else:
                    load_att(h, att_row(b0_as1, h), att_row(b0_ad1, h), D)

            def softmax_and_elu(h, last=False):
                for c in (0, 1):
                    split_hi(act, 2 * h + 1, c)
                att_for(h + 1, last)
                exps(h)
                for c in (2, 3):
                    split_hi(act, 2 * h + 1, c)
                weights_hi(h)
                for c in (4, 5):
                    split_hi(act, 2 * h + 1, c)
                elu(h)

            def head(h, last=False):
                for c in range(CH - 1):
                    split_hi(act, 2 * h, c)
                features_copy(h, 2 * CH * h)
                split_hi(act, 2 * h, CH - 1)
                features_hi(h)
                softmax_and_elu(h, last)

            for c in range(4):
                split_hi(act, 1, c)
            features_copy(0, CH)
            for c in (4, 5):
                split_hi(act, 1, c)
            features_hi(0)
            att_for(1)
            for c in (0, 1, 2):
                split_hi(act, 2, c)
            exps(0)
            split_hi(act, 2, 3)
            weights_hi(0)
            act.wait_ge(h_lo_done, 2)
            features_copy(1, 2 * CH)
            act.wait_ge(b1_ready, 1)
            elu(0, first=True)
            split_hi(act, 2, 4)
            split_hi(act, 2, 5)
            features_hi(1)
            softmax_and_elu(1)
            with act.Fori(2, H0 - 1) as h:
                head(h)
            head(H0 - 1, last=True)

            act.wait_ge(xb_done, NT)
            act.dma_start(rows_d[:, 3, :], b1_br2.partition_broadcast(P)).then_inc(rows_loaded, 16)

            def chunks_hi(first, end):
                for q in plan[first:end]:
                    split_hi1(act, q)

            for i in range(NT):
                features_copy(A_CONV2, CH * PHASES, tile0=1, tiles=(i,))
                features_hi(A_CONV2, tiles=(i,))
            chunks_hi(0, 3)
            exps(A_CONV2)
            load_att(A_GAT1A, b1_as1.rearrange("h c -> (h c)"), b1_ad1.rearrange("h c -> (h c)"), HC)
            chunks_hi(3, 5)
            weights_tiles_hi(A_CONV2)
            chunks_hi(5, 9)
            layer_norm(0, 0, x_sb[:, 0, :], y[0])
            for i in range(NT):
                for part in range(2):
                    act.wait_ge(x1T_ps, 2 * i + part + 1)
                    act.activation(*x1T_part(xT_hi, i, part), ACT.Copy).then_inc(x1T_hi_done, 1)
            features_copy(A_GAT1A, None, tile0=2, tiles=(0,))
            chunks_hi(9, 14)
            features_copy(A_GAT1A, plan[KD - 1]["n"] + 1, tile0=2, tiles=(1,))
            chunks_hi(14, 15)
            features_hi(A_GAT1A)
            chunks_hi(15, 19)
            exps(A_GAT1A)
            features_copy(A_GAT1B, plan[2 * KD - 1]["n"] + 1)
            chunks_hi(19, 21)
            weights_hi(A_GAT1A)
            chunks_hi(21, 22)
            features_hi(A_GAT1B)
            chunks_hi(22, 25)
            act.wait_ge(a_dst_done, before(A_GAT2))
            for half_at, v in ((0, b1_as2), (1, b1_ad2)):
                act.dma_start(att[:, half_at * D:(half_at + 1) * D], v[0:1, :].partition_broadcast(P))\
                   .then_inc(att_loaded, 16)
            exps(A_GAT1B)
            chunks_hi(25, 26)
            weights_hi(A_GAT1B)
            chunks_hi(26, 28)

            def h1_hi(half_at, i):
                act.wait_ge(h1T_ps, NT * half_at + i + 1)
                act.activation(*h1T_part(zT_hi, half_at, i), ACT.Copy).then_inc(h1T_hi_done, 1)

            h1_hi(0, 0)
            chunks_hi(28, 30)
            h1_hi(0, 1)
            chunks_hi(30, 31)
            h1_hi(1, 0)
            chunks_hi(31, 32)
            h1_hi(1, 1)
            chunks_hi(32, 34)
            features_copy(A_GAT2, None, tile0=3, tiles=(0,))
            features_hi(A_GAT2, tiles=(0,))
            features_copy(A_GAT2, plan[4 * KD + KH - 1]["n"] + 1, tile0=3, tiles=(1,))
            chunks_hi(34, 36)
            features_hi(A_GAT2, tiles=(1,))
            chunks_hi(36, 38)
            exps(A_GAT2)
            chunks_hi(38, 40)
            weights_tiles_hi(A_GAT2)
            layer_norm(2, 1, y[1], y[1])
            layer_norm(3, 0, x_sb[:, 0, :], y[0])

        @block.tensor
        def _(pe):
            def pieces(i):
                return ((0, BANK, 0), (BANK, D, BANK)) if i == 0 else ((0, N, D), (N, D, 2 * BANK))

            def product(at, i, lhs_hi, lhs_lo, w_hi, w_lo, start, stop, bank2_wait=None, piece=None):
                last = None
                for n, (a, b) in enumerate(three(lhs_hi, lhs_lo, w_hi, w_lo)):
                    for lo, hi, to in pieces(i) if piece is None else pieces(i)[piece:piece + 1]:
                        if to == 2 * BANK and n == 0 and bank2_wait is not None:
                            pe.wait_ge(*bank2_wait)
                        last = pe.matmul(ps[:, at + to:at + to + hi - lo], a, b[:, lo:hi],
                                         start=start and n == 0 and to != D,
                                         stop=stop and n == PASSES - 1, skip_group_check=True)
                return last

            def chunk(p, c):
                pe.wait_ge(*lo_count(p, c))

            def node_tile(t, k, i):
                return t[:, k, i * P:(i + 1) * P]

            def keep_warm(times, at):
                for _ in range(times):
                    pe.matmul(ps[:, at:at + BANK], zeros[:, 0:P], zeros[:, :], start=True, stop=True)

            def project_chunk(p, h, c, loop=False, at=PROJ):
                chunk(p, c)
                for i in range(NT):
                    wait = (z_done, 6 * h - 4) if c == 0 and i == 1 and loop else None
                    last = product(at, i, node_tile(xT_hi, c, i), node_tile(xT_lo, c, i),
                                   slot_hi(c), slot_lo(c), c == 0, c == CH - 1, wait)
                last.then_inc(chunk_used, 1)

            def accumulate(p, h, c, last_head=False):
                if c % 2 == 0:
                    pe.wait_ge(z_lo_done, 3 * h + c // 2 + 1)
                chunk(p, c)
                for i in range(NT):
                    last = product(ACC, i, node_tile(zT_hi, c, i), node_tile(zT_lo, c, i),
                                   slot_hi(c), slot_lo(c), False, last_head and c == CH - 1)
                last.then_inc(chunk_used, 1)

            def scores(a):
                pe.wait_ge(a_src_done, before(a) + 2 * heads_of(a))
                for k in range(heads_of(a)):
                    for j in range(NT):
                        c, at = 2 * (first_head(a) + k) + j, s_at(a, k) + j * P
                        last = pe.transpose(ps[:, at:at + P], a_s[:, c:c + 1].to_broadcast([P, P]), ident[:, :])
                last.then_inc(scores_bc, 1)

            def weights(a):
                for k in range(heads_of(a)):
                    if scaled_late(a):
                        pe.wait_ge(p_done, before(a) + 2 * (k + 1))
                    else:
                        pe.wait_ge(norm_done, before(a) + 2 * (k + 1))
                    t = e2 if scaled_late(a) else am
                    for j in range(NT):
                        for i in range(NT):
                            at = pT_at(a, k) + j * N + i * P
                            last = pe.transpose(ps[:, at:at + P], t[:, first_head(a) + k, i, j * P:(j + 1) * P],
                                                ident[:, :])
                    last.then_inc(pT_ps, 1)

            def weights_tiles(a):
                for i in range(NT):
                    pe.wait_ge(p_done, before(a) + i + 1)
                    for j in range(NT):
                        last = pe.transpose(ps[:, WT_AT[i] + j * P:WT_AT[i] + (j + 1) * P],
                                            e2[:, 0, i, j * P:(j + 1) * P], ident[:, :])
                    last.then_inc(wt_ps, 1)

            def aggregate_T(h):
                pe.wait_ge(h_lo_done, 2 * h + 2)
                pe.wait_ge(pT_lo_done, h + 1)
                for q in range(3):
                    if elu_at(h, q) == ELU_AT[0] and isinstance(h, int) and h == 0:
                        pe.wait_ge(hs_done, 4)
                    for c in range(2):
                        ch = (2 * q + c) * P
                        at = elu_at(h, q) + c * N
                        for j in range(NT):
                            f = [feat(t, 0, j)[:, ch:ch + P] for t in (h_hi, h_lo)]
                            for n, (a, b) in enumerate(three(*f, pT_hi[:, 0, j, :], pT_lo[:, 0, j, :])):
                                last = pe.matmul(ps[:, at:at + N], a, b,
                                                 start=c == 0 and j == 0 and n == 0,
                                                 stop=j == NT - 1 and n == PASSES - 1, skip_group_check=True)
                    last.then_inc(agg_done, 1)

            def aggregate(a):
                pe.wait_ge(h_lo_done, 2 * a + 2)
                for i in range(NT):
                    pe.wait_ge(wt_lo_done, tiles_before(a) + i + 1)
                    for j in range(NT):
                        w = [t[:, 0, j, i * P:(i + 1) * P] for t in (pT_hi, pT_lo)]
                        for n, (l, r) in enumerate(three(*w, feat(h_hi, a, j), feat(h_lo, a, j))):
                            for lo, hi in ((0, BANK), (BANK, D)):
                                last = pe.matmul(ps[:, NAT_AT[i] + lo:NAT_AT[i] + hi], l, r[:, lo:hi],
                                                 start=j == 0 and n == 0, stop=j == NT - 1 and n == PASSES - 1)
                    last.then_inc(nat_done, 1)

            pe.wait_ge(zeros_set, 1)
            keep_warm(8, PROJ)
            pe.wait_ge(consts, 2)
            pe.wait_ge(x_loaded, 16)
            for b in range(3):
                for k in (2 * b, 2 * b + 1):
                    for i in range(NT):
                        at = 5 * BANK + k * N + i * P
                        last = pe.transpose(ps[:, at:at + P], x_sb[:, i, k * P:(k + 1) * P], ident[:, :])
                last.then_inc(xT_ps, 1)
            pe.wait_ge(b1_loaded, 16)
            pe.transpose(ps[:, BANK:BANK + H0 * KD], b1_rows[:, :], ident[0:H0 * KD, 0:H0 * KD])\
              .then_inc(b1_ps, 1)
            for c in range(CH):
                if c % 2 == 0:
                    pe.wait_ge(xT_lo_done, c // 2 + 1)
                project_chunk(FIRST_PHASE, 0, c, at=ACC)

            def count_edges():
                for i in range(NT):
                    for t in range(ET):
                        if i == 0 and t % per_home == 0:
                            pe.wait_ge(hot_done, 2 * (t + per_home))
                        last = pe.matmul(ps[:, (6 + i) * BANK:(6 + i) * BANK + N], hot(t, 1)[:, i * P:(i + 1) * P],
                                         hot(t, 0), start=t == 0, stop=t == ET - 1)
                    last.then_inc(counted, 1)

            for c in range(CH):
                if c == 0:
                    pe.wait_ge(b1_ready, 1)
                if c == 2:
                    count_edges()
                if c == 3:
                    pe.wait_ge(counts_copied, 2)
                    scores(0)
                project_chunk(1, 1, c)
            weights(0)
            pe.wait_ge(hs_done, NT)
            for b in range(3):
                pe.matmul(ps[:, ACC + b * BANK:ACC + (b + 1) * BANK], zeros[:, 0:P], zeros[:, :],
                          start=True, stop=False, skip_group_check=True)
            aggregate_T(0)

            def rest_of_head(h):
                for c in range(CH):
                    if c == 2:
                        pe.wait_ge(z_done, 6 * h)
                        scores(h)
                    if c == 5:
                        weights(h)
                    accumulate(2 * h, h - 1, c)
                aggregate_T(h)

            rest_of_head(1)
            with pe.Fori(2, H0) as h:
                for c in range(CH):
                    project_chunk(2 * h - 1, h, c, loop=True)
                rest_of_head(h)
            def last_accumulate(c, i, piece=None):
                return product(ACC, i, node_tile(zT_hi, c, i), node_tile(zT_lo, c, i), slot_hi(c), slot_lo(c),
                               False, c == CH - 1, piece=piece)

            for c in range(CH):
                if c % 2 == 0:
                    pe.wait_ge(z_lo_done, 3 * (H0 - 1) + c // 2 + 1)
                chunk(PHASES - 1, c)
                last = last_accumulate(c, 0)
            last.then_inc(tile0_done, 1)
            for c in range(CH):
                last_accumulate(c, 1, piece=1)
            pe.wait_ge(hs_done, 2 * A_CONV2 + 1)
            for c in range(CH):
                last_accumulate(c, 1, piece=0).then_inc(chunk_used, 1)

            pe.wait_ge(z_done, 6 * H0)
            idle = PROJ
            keep_warm(8, idle)
            scores(A_CONV2)
            keep_warm(15, idle)
            weights_tiles(A_CONV2)
            keep_warm(3, idle)
            aggregate(A_CONV2)
            idle = WT_AT[1]
            keep_warm(12, idle)
            def transpose_x1(i):
                if i == 0:
                    pe.wait_ge(act_normed, 1)
                else:
                    pe.wait_ge(x1_done, 1)
                for k in range(KD):
                    at = X1T_AT[i] + k * P
                    last = pe.transpose(ps[:, at:at + P], x_sb[:, i, k * P:(k + 1) * P], ident[:, :])
                    if k + 1 in X1T_PARTS:
                        last.then_inc(x1T_ps, 1)

            transpose_x1(0)
            keep_warm(6, idle)

            def wide_product(q, at, tiles=range(NT)):
                pe.wait_ge(lo_by[q["who"]], q["lo"])
                k, w = q["k"], q["ring_at"]
                for i in tiles:
                    to = at + i * HC + q["part"] * HW
                    for n, (a, b) in enumerate(three(node_tile(xT_hi, k, i), node_tile(xT_lo, k, i),
                                                     ring_hi[:, w:w + HW], ring_lo[:, w:w + HW])):
                        last = pe.matmul(ps[:, to:to + HW], a, b, start=k == 0 and n == 0,
                                         stop=k == KD - 1 and n == PASSES - 1)
                if NT - 1 in tiles:
                    last.then_inc(chunk_used, 1)
                elif k == KD - 1:
                    last.then_inc(tile0_done, 1)

            def narrow_product(q, at, i, **more):
                pe.wait_ge(lo_by[q["who"]], q["lo"])
                k, w = q["k"], q["ring_at"]
                return product(at, i, node_tile(zT_hi, k, i), node_tile(zT_lo, k, i),
                               ring_hi[:, w:w + D], ring_lo[:, w:w + D], k == 0, k == KH - 1, **more)

            w1a, w1b, wr1a, wr1b = (plan[n * KD:(n + 1) * KD] for n in range(4))
            for i in range(NT):
                for q in w1a:
                    if i == 0 and q["k"] == 1:
                        transpose_x1(1)
                    if q["k"] in (0, X1T_PARTS[0]):
                        pe.wait_ge(x1T_lo_done, 2 * i + 1 + (q["k"] > 0))
                    wide_product(q, 0, tiles=(i,))
            for q in w1b:
                if q["k"] == 1:
                    scores(A_GAT1A)
                wide_product(q, 0)

            def aggregate_half(a):
                pe.wait_ge(h_lo_done, 2 * a + 2)
                pe.wait_ge(pT_lo_done, pT_before(a) + HH)
                for i in range(NT):
                    for k in range(HH):
                        for j in range(NT):
                            f = [feat(t, a, j)[:, k * C1:(k + 1) * C1] for t in (h_hi, h_lo)]
                            w = [t[:, first_head(a) + k, j, i * P:(i + 1) * P] for t in (pT_hi, pT_lo)]
                            for n, (l, r) in enumerate(three(*w, *f)):
                                to = i * HC + (a - A_GAT1A) * HW + k * C1
                                last = pe.matmul(ps[:, to:to + C1], l, r, start=k == 0 and j == 0 and n == 0,
                                                 stop=j == NT - 1 and n == PASSES - 1, skip_group_check=True)
                    last.then_inc(nat_done, 1)

            for q in wr1a:
                if q["k"] == 2:
                    weights(A_GAT1A)
                if q["k"] == 4:
                    scores(A_GAT1B)
                wide_product(q, 4 * BANK)
            def transpose_h1(half_at, i):
                pe.wait_ge(h1_done, NT * half_at + i + 1)
                for k in range(H1_PART):
                    at = h1T_at(half_at, i) + k * P
                    ch = i * HC + (half_at * H1_PART + k) * P
                    last = pe.transpose(ps[:, at:at + P], z[:, ch:ch + P], ident[:, :])
                last.then_inc(h1T_ps, 1)

            for q in wr1b:
                if q["k"] == 1:
                    aggregate_half(A_GAT1A)
                    weights(A_GAT1B)
                if q["k"] == 2:
                    aggregate_half(A_GAT1B)
                if q["k"] == 5:
                    transpose_h1(0, 0)
                wide_product(q, 4 * BANK)
            w2 = plan[4 * KD:4 * KD + KH]
            wr2 = plan[4 * KD + KH:]
            pe.wait_ge(h1T_lo_done, 1)
            for q in w2[:H1_PART]:
                if q["k"] == 2:
                    transpose_h1(0, 1)
                narrow_product(q, 0, 0)
            pe.wait_ge(h1T_lo_done, 2)
            for q in w2[:H1_PART]:
                if q["k"] == 2:
                    transpose_h1(1, 0)
                narrow_product(q, 0, 1).then_inc(chunk_used, 1)
            pe.wait_ge(h1T_lo_done, 3)
            for q in w2[H1_PART:]:
                if q["k"] == 6:
                    transpose_h1(1, 1)
                last = narrow_product(q, 0, 0)
            last.then_inc(tile0_done, 1)
            pe.wait_ge(h1T_lo_done, 4)
            for q in w2[H1_PART:]:
                narrow_product(q, 0, 1, piece=1)
            pe.wait_ge(hs_done, 2 * A_GAT2 + 1)
            for q in w2[H1_PART:]:
                narrow_product(q, 0, 1, piece=0).then_inc(chunk_used, 1)
            for q in wr2[:H1_PART]:
                if q["k"] == 1:
                    scores(A_GAT2)
                for i in range(NT):
                    if q["k"] == H1_PART - 1 and i == 1:
                        weights_tiles(A_GAT2)
                    last = narrow_product(q, 3 * BANK, i)
                last.then_inc(chunk_used, 1)
            aggregate(A_GAT2)
            for q in wr2[H1_PART:]:
                last = narrow_product(q, 3 * BANK, 0)
            last.then_inc(tile0_done, 1)
            for q in wr2[H1_PART:]:
                narrow_product(q, 3 * BANK, 1, piece=1)
            pe.wait_ge(r2_added, 1)
            for q in wr2[H1_PART:]:
                narrow_product(q, 3 * BANK, 1, piece=0).then_inc(chunk_used, 1)

        @block.vector
        def _(dve):
            def input_lo(b):
                dve.wait_ge(xT_hi_done, b + 1)
                dve.tensor_tensor(xT_lo[:, 2 * b:2 * b + 2, :].rearrange("p k n -> p (k n)"),
                                  ps[:, (5 + b) * BANK:(6 + b) * BANK],
                                  xT_hi[:, 2 * b:2 * b + 2, :].rearrange("p k n -> p (k n)").bitcast(F32),
                                  ALU.subtract).then_inc(xT_lo_done, 1)

            dve.wait_ge(iota_ready, 1)
            dve.tensor_copy(iota[:, :], iota_i).then_inc(edges_cast, 1)
            input_lo(0)
            split_lo(dve, FIRST_PHASE, 0)
            input_lo(1)
            input_lo(2)
            dve.wait_ge(edges_loaded, 32)
            dve.tensor_copy(edges_f[:, :, :], edges[:, :, :]).then_inc(edges_cast, 1)
            dve.wait_ge(b1_ps, 1)
            dve.tensor_copy(b1_cols[:, :], ps[:, BANK:BANK + H0 * KD]).then_inc(b1_ready, 1)
            dve.wait_ge(edges_cast, 2)
            for t in range(ET):
                for which in range(2):
                    dve.tensor_scalar(hot(t, which), iota[:, :], edges_f[:, which, t:t + 1], None,
                                      ALU.is_equal).then_inc(hot_done, 1)
                if t == per_home - 1:
                    for c in range(POOL_CH, CH):
                        split_lo(dve, FIRST_PHASE, c)

            def dots(a, t, half_at, done, tiles=range(NT)):
                n = heads_of(a)
                w, row = (C1, HC) if n > 1 else (D, D)
                junk = (e1, e2)[half_at][:].rearrange("p a b c -> p (a b c)")
                for i in tiles:
                    if half_at == 0:
                        dve.wait_ge(hs_done, 2 * a + i + 1)
                    for k in range(first_head(a), first_head(a) + n):
                        at = (k * NT + i) * w if n > 1 else i * D
                        dve.tensor_tensor_reduce(junk[:, at:at + w],
                                                 feat(hs, a, i)[:, (k - first_head(a)) * w:(k - first_head(a) + 1) * w],
                                                 att[:, half_at * row + k * w:half_at * row + (k + 1) * w],
                                                 1.0, 0.0, ALU.mult, ALU.add, t[:, 2 * k + i:2 * k + i + 1])\
                           .then_inc(done, 1)

            def both_dots(a, between=()):
                pairs = a + 1 if not isinstance(a, int) or a < A_GAT1B else a
                dve.wait_ge(att_loaded, 32 * pairs)
                if isinstance(a, int) and a in (A_CONV2, A_GAT1A, A_GAT2):
                    for i in range(NT):
                        dots(a, a_s, 0, a_src_done, tiles=(i,))
                        dots(a, a_d, 1, a_dst_done, tiles=(i,))
                        for q in between if i == 0 else ():
                            split_lo1(dve, q)
                else:
                    dots(a, a_s, 0, a_src_done)
                    dots(a, a_d, 1, a_dst_done)

            def maxima(a):
                upto = before(a) + 2 * heads_of(a)
                first = first_head(a)
                small = slice(2 * first, 2 * (first + heads_of(a)))
                dve.wait_ge(a_dst_done, upto)
                dve.wait_ge(scores_bc, a + 1)
                dve.tensor_scalar(a_d2[:, small], a_d[:, small], SLOPE, None, ALU.mult)
                for k in range(heads_of(a)):
                    for i in range(NT):
                        c = 2 * (first + k) + i
                        dve.tensor_tensor_reduce(am[:, first + k, i, :], ps[:, s_at(a, k):s_at(a, k) + N],
                                                 far[:, i, :], 1.0, -3.0e38, ALU.add, ALU.max, mx[:, c:c + 1])\
                           .then_inc(masked, 1)
                dve.wait_ge(masked, upto)
                dve.tensor_tensor(zc[:, small], mx[:, small], a_d[:, small], ALU.add).then_inc(top_done, 1)
                dve.wait_ge(top_done, a + 1)
                dve.scalar_tensor_tensor(mm[:, small], zc[:, small], SLOPE, zc[:, small], ALU.mult, ALU.max)\
                   .then_inc(m_done, 1)
                dve.wait_ge(m_done, a + 1)
                dve.tensor_tensor(bias1[:, small], a_d[:, small], mm[:, small], ALU.subtract).then_inc(bias_done, 1)
                dve.tensor_tensor(bias2[:, small], a_d2[:, small], mm[:, small], ALU.subtract).then_inc(bias_done, 1)

            def normalise(a):
                def greater(g, k, i):
                    dve.wait_ge(exps_done, 2 * before(a) + 4 * k + 2 * (i + 1))
                    dve.tensor_tensor(e1[:, g, i, :], e1[:, g, i, :], e2[:, g, i, :], ALU.max)\
                       .then_inc(emax_done, 1)

                by_tile = scaled_late(a) and heads_of(a) == 1
                for k in range(heads_of(a)):
                    g = first_head(a) + k
                    for i in () if by_tile else range(NT):
                        greater(g, k, i)
                    for i in range(NT):
                        c = 2 * g + i
                        if by_tile:
                            greater(g, k, i)
                        dve.wait_ge(emax_done, before(a) + 2 * k + i + 1)
                        dve.scalar_tensor_tensor(e2[:, g, i, :], e1[:, g, i, :], 1.0, counts[:, i, :], ALU.mult,
                                                 ALU.mult, accum_out=zsum[:, c:c + 1]).then_inc(p_done, 1)
                if scaled_late(a):
                    return
                inverse_sums(a)
                dve.wait_ge(rz_done, a + 1)
                for i in range(NT):
                    dve.tensor_scalar(am[:, 0, i, :], e2[:, 0, i, :], rz[:, i:i + 1], None,
                                      ALU.mult).then_inc(norm_done, 1)

            def inverse_sums(a):
                dve.wait_ge(p_done, before(a) + 2 * heads_of(a))
                small = slice(2 * first_head(a), 2 * (first_head(a) + heads_of(a)))
                dve.reciprocal(rz[:, small], zsum[:, small]).then_inc(rz_done, 1)

            def weights_lo(a):
                for k in range(heads_of(a)):
                    dve.wait_ge(pT_hi_done, pT_before(a) + k + 1)
                    at = pT_at(a, k)
                    g = first_head(a) + k
                    dve.tensor_tensor(pT_lo[:, g, :, :].rearrange("p j n -> p (j n)"), ps[:, at:at + 2 * N],
                                      pT_hi[:, g, :, :].rearrange("p j n -> p (j n)").bitcast(F32),
                                      ALU.subtract).then_inc(pT_lo_done, 1)

            def weights_tiles_lo(a):
                for i in range(NT):
                    dve.wait_ge(wt_hi_done, tiles_before(a) + i + 1)
                    to, transposed = weights_tile(pT_lo, i)
                    dve.tensor_tensor(to, transposed, weights_tile(pT_hi, i)[0].bitcast(F32), ALU.subtract)\
                       .then_inc(wt_lo_done, 1)

            def elu(h):
                for q in range(3):
                    pair = z[:, 2 * q * N:(2 * q + 2) * N]
                    dve.wait_ge(elu_exp, 6 * h + 2 * q + 2)
                    dve.tensor_scalar(pair, pair, 1.0, -1.0, ALU.min, ALU.add).then_inc(elu_neg, 1)
                    dve.wait_ge(elu_neg, 3 * h + q + 1)
                    for c in range(2):
                        t = 2 * q + c
                        dve.scalar_tensor_tensor(z[:, t * N:(t + 1) * N],
                                                 ps[:, elu_at(h, q) + c * N:elu_at(h, q) + (c + 1) * N],
                                                 b1_cols[:, bass.ds(KD * h + t, 1)], z[:, t * N:(t + 1) * N],
                                                 ALU.add, ALU.max).then_inc(z_done, 1)
                    if q >= 1:
                        elu_lo(h, q - 1)
                elu_lo(h, 2)

            def elu_lo(h, q):
                dve.wait_ge(z_hi_done, 3 * h + q + 1)
                hi = zT_hi[:, 2 * q:2 * q + 2, :].rearrange("p k n -> p (k n)")
                dve.tensor_tensor(zT_lo[:, 2 * q:2 * q + 2, :].rearrange("p k n -> p (k n)"),
                                  z[:, 2 * q * N:(2 * q + 2) * N], hi.bitcast(F32), ALU.subtract)\
                   .then_inc(z_lo_done, 1)

            for c in range(POOL_CH, CH):
                split_lo(dve, 1, c)
            both_dots(0)
            for i in range(NT):
                dve.wait_ge(counted, i + 1)
                dve.tensor_copy(counts[:, i, :], ps[:, (6 + i) * BANK:(6 + i) * BANK + N]).then_inc(counts_copied, 1)
            dve.wait_ge(counts_copied, NT)
            for i in range(NT):
                loops = counts[:, i, i * P:(i + 1) * P]
                dve.tensor_tensor(loops, loops, ident[:, :], ALU.add).then_inc(counts_done, 1)
            dve.wait_ge(counts_done, NT)
            dve.tensor_scalar(far[:, :, :], counts[:, :, :], 0.0, FAR, ALU.is_equal, ALU.mult).then_inc(far_done, 1)
            dve.wait_ge(far_done, 1)

            def softmax_and_elu(h, phase=None, dotted=False):
                if not dotted:
                    both_dots(h)
                maxima(h)
                if phase is not None:
                    split_lo(dve, phase, CH - 1)
                normalise(h)
                weights_lo(h)
                for c in range(POOL_CH, CH):
                    split_lo(dve, 2 * h + 1, c)
                elu(h)

            maxima(0)
            normalise(0)
            weights_lo(0)
            dve.wait_ge(att_loaded, 32 * 2)
            dots(1, a_s, 0, a_src_done)
            elu(0)
            split_lo(dve, 2, POOL_CH)
            dots(1, a_d, 1, a_dst_done)
            softmax_and_elu(1, phase=2, dotted=True)
            with dve.Fori(2, H0) as h:
                split_lo(dve, 2 * h, POOL_CH)
                softmax_and_elu(h, phase=2 * h)

            def layer_mean(n, i, parts):
                dve.wait_ge(stats_done, parts)
                dve.bn_aggr(mv[:, i, :], stats[:, i, :, :]).then_inc(aggr_done, 1)
                dve.wait_ge(aggr_done, NT * n + i + 1)
                if (n, i) in ON_ACT:
                    dve.tensor_scalar(minus_mean[:, i:i + 1], mv[:, i, 0:1], -1.0, None, ALU.mult)\
                       .then_inc(minus_mean_done, 1)
                dve.tensor_scalar(ve[:, i:i + 1], mv[:, i, 1:2], EPS, None, ALU.add).then_inc(ve_done, 1)

            def layer_stats(n, i, t, width):
                part = width // 2
                for s in range(2):
                    dve.bn_stats(stats[:, i, s, :], t[:, s * part:(s + 1) * part]).then_inc(stats_done, 1)
                layer_mean(n, i, 2 * (NT * n + i + 1))

            mine = [q for q in plan if q["who"] == "dve"]
            both_dots(A_CONV2)
            maxima(A_CONV2)
            normalise(A_CONV2)
            weights_tiles_lo(A_CONV2)
            inverse_sums(A_CONV2)
            y = [z[:, i * D:(i + 1) * D] for i in range(NT)]
            dve.wait_ge(xb_done, NT)
            dve.wait_ge(rz_done, A_CONV2 + 1)
            def x1_lo(i, part):
                dve.wait_ge(x1T_hi_done, 2 * i + part + 1)
                to, transposed = x1T_part(xT_lo, i, part)
                dve.tensor_tensor(to, transposed, x1T_part(xT_hi, i, part)[0].bitcast(F32), ALU.subtract)\
                   .then_inc(x1T_lo_done, 1)

            for i in range(NT):
                dve.wait_ge(nat_done, i + 1)
                dve.scalar_tensor_tensor(y[i], ps[:, NAT_AT[i]:NAT_AT[i] + D], rz[:, i:i + 1], x_sb[:, i, :],
                                         ALU.mult, ALU.add).then_inc(biased, 1)
                dve.wait_ge(biased, i + 1)
                layer_stats(0, i, y[i], D)
            dve.wait_ge(rstd_done, 2)
            dve.tensor_scalar(x_sb[:, 1, :], y[1], mv[:, 1, 0:1], rstd[:, 1:2], ALU.subtract, ALU.mult)\
               .then_inc(x1_done, 1)
            x1_lo(0, 0)
            x1_lo(0, 1)
            for q in mine[:3]:
                split_lo1(dve, q)
            x1_lo(1, 0)
            x1_lo(1, 1)

            def columns(half_at):
                return slice(half_at * HW, (half_at + 1) * HW)

            def residual(half_at):
                dve.wait_ge(chunk_used, plan[(3 + half_at) * KD - 1]["n"] + 1)
                dve.wait_ge(h_lo_done, 2 * (A_GAT1A + half_at) + 2)
                for i in range(NT):
                    at = 4 * BANK + i * HC + half_at * HW
                    dve.tensor_tensor(hs[:, at - 4 * BANK:at - 4 * BANK + HW], ps[:, at:at + HW],
                                      rows_hc[:, 3, columns(half_at)], ALU.add).then_inc(r_added, 1)

            both_dots(A_GAT1A, between=mine[3:6])
            maxima(A_GAT1A)
            normalise(A_GAT1A)
            both_dots(A_GAT1B)
            maxima(A_GAT1B)
            weights_lo(A_GAT1A)
            inverse_sums(A_GAT1A)
            dve.wait_ge(rows_loaded, 16 * 8)
            residual(0)
            normalise(A_GAT1B)

            y1 = [z[:, i * HC:(i + 1) * HC] for i in range(NT)]

            def biased_half(half_at, i):
                a = A_GAT1A + half_at
                dve.wait_ge(nat_done, 2 * NT + i + 1 - NT * (1 - half_at))
                for k in range(first_head(a), first_head(a) + HH):
                    dve.scalar_tensor_tensor(y1[i][:, k * C1:(k + 1) * C1],
                                             ps[:, i * HC + k * C1:i * HC + (k + 1) * C1],
                                             rz[:, 2 * k + i:2 * k + i + 1], rows_hc[:, 0, k * C1:(k + 1) * C1],
                                             ALU.mult, ALU.add).then_inc(biased, 1)
                dve.wait_ge(biased, NT + HH * (NT * half_at + i + 1))
                dve.bn_stats(stats[:, i, half_at, :], y1[i][:, columns(half_at)]).then_inc(stats_done, 1)

            dve.wait_ge(rz_done, A_GAT1A + 1)
            biased_half(0, 0)
            weights_lo(A_GAT1B)
            biased_half(0, 1)
            inverse_sums(A_GAT1B)
            dve.wait_ge(rz_done, A_GAT1B + 1)

            def h1_half(half_at, i):
                cols, n = columns(half_at), NT * half_at + i + 1
                t = y1[i][:, cols]
                dve.scalar_tensor_tensor(t, t, mv[:, i, 0:1], rows_hc[:, 1, cols],
                                         ALU.subtract, ALU.mult).then_inc(norm1, 1)
                dve.wait_ge(norm1, n)
                dve.wait_ge(rstd_done, NT + i + 1)
                dve.scalar_tensor_tensor(t, t, rstd[:, i:i + 1], rows_hc[:, 2, cols],
                                         ALU.mult, ALU.add).then_inc(norm2, 1)
                dve.wait_ge(norm2, n)
                dve.wait_ge(r_added, NT * half_at + i + 1)
                at = i * HC + half_at * HW
                dve.scalar_tensor_tensor(t, t, 0.0, hs[:, at:at + HW], ALU.max, ALU.add).then_inc(h1_done, 1)

            def h1_lo(half_at, i):
                dve.wait_ge(h1T_hi_done, NT * half_at + i + 1)
                to, transposed = h1T_part(zT_lo, half_at, i)
                dve.tensor_tensor(to, transposed, h1T_part(zT_hi, half_at, i)[0].bitcast(F32), ALU.subtract)\
                   .then_inc(h1T_lo_done, 1)

            biased_half(1, 0)
            layer_mean(1, 0, 3 * NT + 1)
            h1_half(0, 0)
            biased_half(1, 1)
            h1_lo(0, 0)
            layer_mean(1, 1, 3 * NT + 2)
            h1_half(0, 1)
            residual(1)
            h1_lo(0, 1)
            h1_half(1, 0)
            split_lo1(dve, mine[6])
            h1_lo(1, 0)
            h1_half(1, 1)
            split_lo1(dve, mine[7])
            h1_lo(1, 1)
            both_dots(A_GAT2)
            maxima(A_GAT2)
            normalise(A_GAT2)
            weights_tiles_lo(A_GAT2)
            inverse_sums(A_GAT2)
            for q in mine[8:]:
                split_lo1(dve, q)
            dve.wait_ge(rz_done, A_GAT2 + 1)
            for i in range(NT):
                dve.wait_ge(nat_done, 3 * NT + i + 1)
                dve.scalar_tensor_tensor(y[i], ps[:, NAT_AT[i]:NAT_AT[i] + D], rz[:, i:i + 1], rows_d[:, 0, :],
                                         ALU.mult, ALU.add).then_inc(biased, 1)
                dve.wait_ge(biased, NT + 2 * H1 + i + 1)
                layer_stats(2, i, y[i], D)
            for i in range(NT):
                dve.wait_ge(shifted, i + 1)
                if i == 0:
                    dve.scalar_tensor_tensor(y[i], y[i], mv[:, i, 0:1], rows_d[:, 1, :], ALU.subtract, ALU.mult)\
                       .then_inc(norm1, 1)
                    dve.wait_ge(norm1, 2 * NT + 1)
                    dve.wait_ge(rstd_done, 2 * NT + 1)
                    dve.scalar_tensor_tensor(y[i], y[i], rstd[:, i:i + 1], shift(i), ALU.mult, ALU.add)\
                       .then_inc(norm2, 1)
                else:
                    dve.wait_ge(scaled, 1)
                    dve.tensor_tensor(y[i], y[i], shift(i), ALU.add).then_inc(norm2, 1)
                dve.wait_ge(norm2, 2 * NT + i + 1)
                if i == 0:
                    dve.wait_ge(tile0_done, 4)
                else:
                    dve.wait_ge(chunk_used, plan[-1]["n"] + 1)
                dve.tensor_tensor(y[i], ps[:, 3 * BANK + i * D:3 * BANK + (i + 1) * D], y[i], ALU.add)\
                   .then_inc(r2_added, 1)
                dve.wait_ge(r2_added, i + 1)
                layer_stats(3, i, y[i], D)
            dve.wait_ge(rstd_done, 3 * NT + 2)
            for cols in OUT_HALVES:
                dve.tensor_scalar(x_sb[:, 1, cols], y[1][:, cols], mv[:, 1, 0:1], rstd[:, 1:2],
                                  ALU.subtract, ALU.mult).then_inc(out_ready, 1)


INPUTS = ["x", "src", "dst"] \
    + ["L0_gnn_" + n for n in ("W1", "a_src1", "a_dst1", "b1", "W2", "a_src2", "a_dst2", "b2")] \
    + ["L1_gnn_" + n for n in ("W1", "a_src1", "a_dst1", "b1", "g1", "be1", "Wr1", "br1",
                               "W2", "a_src2", "a_dst2", "b2", "g2", "be2", "Wr2", "br2")]


def kernel(**inputs):
    import numpy as np
    import concourse.bacc as bacc
    from concourse.bass_utils import run_bass_kernel_spmd

    nc = bacc.Bacc("TRN2", target_bir_lowering=False, num_devices=1)
    arrays, args = {}, []
    for name in INPUTS:
        a = np.ascontiguousarray(inputs[name])
        arrays[f"in_{name}"] = a
        args.append(nc.dram_tensor(f"in_{name}", a.shape, mybir.dt.from_np(a.dtype), kind="ExternalInput").ap())
    out = nc.dram_tensor("out", (N, D), F32, kind="ExternalOutput").ap()
    build_gnn(nc, *args, out)
    r = run_bass_kernel_spmd(nc, [arrays], core_ids=[0])
    return r.results[0]["out"]
```
